# Optimizing a Trainium2 kernel written in Bass

```python
import numpy as np
import jax
import jax.numpy as jnp

def _softmax(x, axis=-1):
    return jax.nn.softmax(x, axis=axis)

def _gelu(x):
    return jax.nn.gelu(x, approximate=True)

def _silu(x):
    return jax.nn.silu(x)

def _sigmoid(x):
    return jax.nn.sigmoid(x)

def _layernorm(x, axis=-1, eps=1e-05):
    m = jnp.mean(x, axis=axis, keepdims=True)
    v = jnp.var(x, axis=axis, keepdims=True)
    return (x - m) / jnp.sqrt(v + eps)

def _scatter_add(tgt, idx, src, axis=0):
    return tgt.at[idx].add(src)

def _segment_sum(src, seg, n):
    return jax.ops.segment_sum(src, seg, n)
kernel_name = 'mk_dlrm_tower_d1_rec_r8_d3adf9'

def setup_inputs(seed: int=0):
    np.random.seed(seed)
    _w = jnp.asarray

    def _rec_inputs():
        import jax
        import jax.numpy as jnp
        _tk = jax.random.key(seed)
        dense_ctx = jax.random.normal(jax.random.fold_in(_tk, 190), (1024, 16), jnp.float32)
        ids = jnp.stack([jax.random.randint(jax.random.fold_in(_tk, 200 + f), (1024,), 0, v, jnp.int32) for f, v in enumerate([12500, 125000, 1250, 1000, 1250, 1250, 1000, 1000, 125000, 12500, 1250, 1250, 1000, 12500, 125000, 125000, 12500, 125000, 12500, 1250, 1250, 1250, 1000, 12500, 1000, 125000, 1250, 1250, 12500, 12500, 125000, 1250, 125000, 12500, 125000, 12500, 1000, 125000, 12500])], axis=1)
        tbl_0 = 0.05 * jax.random.normal(jax.random.fold_in(_tk, 500 + 0), (12500, 16), jnp.float32)
        tbl_1 = 0.05 * jax.random.normal(jax.random.fold_in(_tk, 500 + 1), (125000, 16), jnp.float32)
        tbl_2 = 0.05 * jax.random.normal(jax.random.fold_in(_tk, 500 + 2), (1250, 16), jnp.float32)
        tbl_3 = 0.05 * jax.random.normal(jax.random.fold_in(_tk, 500 + 3), (1000, 16), jnp.float32)
        tbl_4 = 0.05 * jax.random.normal(jax.random.fold_in(_tk, 500 + 4), (1250, 16), jnp.float32)
        tbl_5 = 0.05 * jax.random.normal(jax.random.fold_in(_tk, 500 + 5), (1250, 16), jnp.float32)
        tbl_6 = 0.05 * jax.random.normal(jax.random.fold_in(_tk, 500 + 6), (1000, 16), jnp.float32)
        tbl_7 = 0.05 * jax.random.normal(jax.random.fold_in(_tk, 500 + 7), (1000, 16), jnp.float32)
        tbl_8 = 0.05 * jax.random.normal(jax.random.fold_in(_tk, 500 + 8), (125000, 16), jnp.float32)
        tbl_9 = 0.05 * jax.random.normal(jax.random.fold_in(_tk, 500 + 9), (12500, 16), jnp.float32)
        tbl_10 = 0.05 * jax.random.normal(jax.random.fold_in(_tk, 500 + 10), (1250, 16), jnp.float32)
        tbl_11 = 0.05 * jax.random.normal(jax.random.fold_in(_tk, 500 + 11), (1250, 16), jnp.float32)
        tbl_12 = 0.05 * jax.random.normal(jax.random.fold_in(_tk, 500 + 12), (1000, 16), jnp.float32)
        tbl_13 = 0.05 * jax.random.normal(jax.random.fold_in(_tk, 500 + 13), (12500, 16), jnp.float32)
        tbl_14 = 0.05 * jax.random.normal(jax.random.fold_in(_tk, 500 + 14), (125000, 16), jnp.float32)
        tbl_15 = 0.05 * jax.random.normal(jax.random.fold_in(_tk, 500 + 15), (125000, 16), jnp.float32)
        tbl_16 = 0.05 * jax.random.normal(jax.random.fold_in(_tk, 500 + 16), (12500, 16), jnp.float32)
        tbl_17 = 0.05 * jax.random.normal(jax.random.fold_in(_tk, 500 + 17), (125000, 16), jnp.float32)
        tbl_18 = 0.05 * jax.random.normal(jax.random.fold_in(_tk, 500 + 18), (12500, 16), jnp.float32)
        tbl_19 = 0.05 * jax.random.normal(jax.random.fold_in(_tk, 500 + 19), (1250, 16), jnp.float32)
        tbl_20 = 0.05 * jax.random.normal(jax.random.fold_in(_tk, 500 + 20), (1250, 16), jnp.float32)
        tbl_21 = 0.05 * jax.random.normal(jax.random.fold_in(_tk, 500 + 21), (1250, 16), jnp.float32)
        tbl_22 = 0.05 * jax.random.normal(jax.random.fold_in(_tk, 500 + 22), (1000, 16), jnp.float32)
        tbl_23 = 0.05 * jax.random.normal(jax.random.fold_in(_tk, 500 + 23), (12500, 16), jnp.float32)
        tbl_24 = 0.05 * jax.random.normal(jax.random.fold_in(_tk, 500 + 24), (1000, 16), jnp.float32)
        tbl_25 = 0.05 * jax.random.normal(jax.random.fold_in(_tk, 500 + 25), (125000, 16), jnp.float32)
        tbl_26 = 0.05 * jax.random.normal(jax.random.fold_in(_tk, 500 + 26), (1250, 16), jnp.float32)
        tbl_27 = 0.05 * jax.random.normal(jax.random.fold_in(_tk, 500 + 27), (1250, 16), jnp.float32)
        tbl_28 = 0.05 * jax.random.normal(jax.random.fold_in(_tk, 500 + 28), (12500, 16), jnp.float32)
        tbl_29 = 0.05 * jax.random.normal(jax.random.fold_in(_tk, 500 + 29), (12500, 16), jnp.float32)
        tbl_30 = 0.05 * jax.random.normal(jax.random.fold_in(_tk, 500 + 30), (125000, 16), jnp.float32)
        tbl_31 = 0.05 * jax.random.normal(jax.random.fold_in(_tk, 500 + 31), (1250, 16), jnp.float32)
        tbl_32 = 0.05 * jax.random.normal(jax.random.fold_in(_tk, 500 + 32), (125000, 16), jnp.float32)
        tbl_33 = 0.05 * jax.random.normal(jax.random.fold_in(_tk, 500 + 33), (12500, 16), jnp.float32)
        tbl_34 = 0.05 * jax.random.normal(jax.random.fold_in(_tk, 500 + 34), (125000, 16), jnp.float32)
        tbl_35 = 0.05 * jax.random.normal(jax.random.fold_in(_tk, 500 + 35), (12500, 16), jnp.float32)
        tbl_36 = 0.05 * jax.random.normal(jax.random.fold_in(_tk, 500 + 36), (1000, 16), jnp.float32)
        tbl_37 = 0.05 * jax.random.normal(jax.random.fold_in(_tk, 500 + 37), (125000, 16), jnp.float32)
        tbl_38 = 0.05 * jax.random.normal(jax.random.fold_in(_tk, 500 + 38), (12500, 16), jnp.float32)
        _rk = jax.random.fold_in(_tk, 7)
        W_top1 = 0.0606339 * jax.random.normal(jax.random.fold_in(_tk, 801), (272, 512), jnp.float32)
        W_top2 = 0.0441942 * jax.random.normal(jax.random.fold_in(_tk, 802), (512, 256), jnp.float32)
        W_top3 = 0.0625 * jax.random.normal(jax.random.fold_in(_tk, 803), (256, 1), jnp.float32)
        b_top1 = jnp.zeros((512,), jnp.float32)
        b_top2 = jnp.zeros((256,), jnp.float32)
        return (dense_ctx, ids, tbl_0, tbl_1, tbl_2, tbl_3, tbl_4, tbl_5, tbl_6, tbl_7, tbl_8, tbl_9, tbl_10, tbl_11, tbl_12, tbl_13, tbl_14, tbl_15, tbl_16, tbl_17, tbl_18, tbl_19, tbl_20, tbl_21, tbl_22, tbl_23, tbl_24, tbl_25, tbl_26, tbl_27, tbl_28, tbl_29, tbl_30, tbl_31, tbl_32, tbl_33, tbl_34, tbl_35, tbl_36, tbl_37, tbl_38, W_top1, b_top1, W_top2, b_top2, W_top3)
    dense_ctx, ids, tbl_0, tbl_1, tbl_2, tbl_3, tbl_4, tbl_5, tbl_6, tbl_7, tbl_8, tbl_9, tbl_10, tbl_11, tbl_12, tbl_13, tbl_14, tbl_15, tbl_16, tbl_17, tbl_18, tbl_19, tbl_20, tbl_21, tbl_22, tbl_23, tbl_24, tbl_25, tbl_26, tbl_27, tbl_28, tbl_29, tbl_30, tbl_31, tbl_32, tbl_33, tbl_34, tbl_35, tbl_36, tbl_37, tbl_38, W_top1, b_top1, W_top2, b_top2, W_top3 = _rec_inputs()

    def _L0_rec_setup():
        import jax, jax.numpy as jnp
        import numpy as np
        B, M0, D = (256, 39, 16)
        CIN_SIZE = [128, 128]

        def _cin(inputs, weights):
            X0 = inputs
            Xi = inputs
            res = []
            for W in weights:
                mi = Xi.shape[1]
                z = jnp.einsum('bmd,bnd->bdmn', X0, Xi)
                z = z.reshape(z.shape[0], z.shape[1], M0 * mi)
                Xi = jnp.einsum('bdp,po->bod', z, W)
                res.append(Xi)
            res = jnp.concatenate(res, axis=1)
            return jnp.sum(res, axis=-1)
        key = jax.random.key(seed)
        k1, k2, k3 = jax.random.split(key, 3)
        inputs = jax.random.normal(k1, (B, M0, D), dtype=jnp.float32)
        W0 = jax.random.normal(k2, (M0 * M0, CIN_SIZE[0]), dtype=jnp.float32) * 0.05
        W1 = jax.random.normal(k3, (M0 * CIN_SIZE[0], CIN_SIZE[1]), dtype=jnp.float32) * 0.05
        return {'inputs': inputs, 'W0': W0, 'W1': W1}
    _L0_rec_all = _L0_rec_setup()
    _L0_rec_in = {k: v for k, v in _L0_rec_all.items() if k in ('W0', 'W1')}
    del _L0_rec_all
    return {'dense_ctx': dense_ctx, 'ids': ids, 'tbl_0': tbl_0, 'tbl_1': tbl_1, 'tbl_2': tbl_2, 'tbl_3': tbl_3, 'tbl_4': tbl_4, 'tbl_5': tbl_5, 'tbl_6': tbl_6, 'tbl_7': tbl_7, 'tbl_8': tbl_8, 'tbl_9': tbl_9, 'tbl_10': tbl_10, 'tbl_11': tbl_11, 'tbl_12': tbl_12, 'tbl_13': tbl_13, 'tbl_14': tbl_14, 'tbl_15': tbl_15, 'tbl_16': tbl_16, 'tbl_17': tbl_17, 'tbl_18': tbl_18, 'tbl_19': tbl_19, 'tbl_20': tbl_20, 'tbl_21': tbl_21, 'tbl_22': tbl_22, 'tbl_23': tbl_23, 'tbl_24': tbl_24, 'tbl_25': tbl_25, 'tbl_26': tbl_26, 'tbl_27': tbl_27, 'tbl_28': tbl_28, 'tbl_29': tbl_29, 'tbl_30': tbl_30, 'tbl_31': tbl_31, 'tbl_32': tbl_32, 'tbl_33': tbl_33, 'tbl_34': tbl_34, 'tbl_35': tbl_35, 'tbl_36': tbl_36, 'tbl_37': tbl_37, 'tbl_38': tbl_38, 'W_top1': W_top1, 'b_top1': b_top1, 'W_top2': W_top2, 'b_top2': b_top2, 'W_top3': W_top3, 'L0_rec_W0': _L0_rec_in['W0'], 'L0_rec_W1': _L0_rec_in['W1']}

def reference(dense_ctx, ids, tbl_0, tbl_1, tbl_2, tbl_3, tbl_4, tbl_5, tbl_6, tbl_7, tbl_8, tbl_9, tbl_10, tbl_11, tbl_12, tbl_13, tbl_14, tbl_15, tbl_16, tbl_17, tbl_18, tbl_19, tbl_20, tbl_21, tbl_22, tbl_23, tbl_24, tbl_25, tbl_26, tbl_27, tbl_28, tbl_29, tbl_30, tbl_31, tbl_32, tbl_33, tbl_34, tbl_35, tbl_36, tbl_37, tbl_38, W_top1, b_top1, W_top2, b_top2, W_top3, L0_rec_W0, L0_rec_W1):
    import jax
    import jax.numpy as jnp

    def _L0_rec_ref(inputs, W0, W1):
        import jax, jax.numpy as jnp
        import numpy as np
        B, M0, D = (256, 39, 16)
        CIN_SIZE = [128, 128]

        def _cin(inputs, weights):
            X0 = inputs
            Xi = inputs
            res = []
            for W in weights:
                mi = Xi.shape[1]
                z = jnp.einsum('bmd,bnd->bdmn', X0, Xi)
                z = z.reshape(z.shape[0], z.shape[1], M0 * mi)
                Xi = jnp.einsum('bdp,po->bod', z, W)
                res.append(Xi)
            res = jnp.concatenate(res, axis=1)
            return jnp.sum(res, axis=-1)
        return _cin(inputs, [W0, W1])
    e = jnp.stack([tbl_0[ids[:, 0]], tbl_1[ids[:, 1]], tbl_2[ids[:, 2]], tbl_3[ids[:, 3]], tbl_4[ids[:, 4]], tbl_5[ids[:, 5]], tbl_6[ids[:, 6]], tbl_7[ids[:, 7]], tbl_8[ids[:, 8]], tbl_9[ids[:, 9]], tbl_10[ids[:, 10]], tbl_11[ids[:, 11]], tbl_12[ids[:, 12]], tbl_13[ids[:, 13]], tbl_14[ids[:, 14]], tbl_15[ids[:, 15]], tbl_16[ids[:, 16]], tbl_17[ids[:, 17]], tbl_18[ids[:, 18]], tbl_19[ids[:, 19]], tbl_20[ids[:, 20]], tbl_21[ids[:, 21]], tbl_22[ids[:, 22]], tbl_23[ids[:, 23]], tbl_24[ids[:, 24]], tbl_25[ids[:, 25]], tbl_26[ids[:, 26]], tbl_27[ids[:, 27]], tbl_28[ids[:, 28]], tbl_29[ids[:, 29]], tbl_30[ids[:, 30]], tbl_31[ids[:, 31]], tbl_32[ids[:, 32]], tbl_33[ids[:, 33]], tbl_34[ids[:, 34]], tbl_35[ids[:, 35]], tbl_36[ids[:, 36]], tbl_37[ids[:, 37]], tbl_38[ids[:, 38]]], axis=1)
    z = _L0_rec_ref(e, L0_rec_W0, L0_rec_W1)
    z = z.reshape(z.shape[0], -1)
    h = jnp.concatenate([z, dense_ctx], axis=1)
    h = jnp.maximum(h @ W_top1 + b_top1, 0.0)
    h = jnp.maximum(h @ W_top2 + b_top2, 0.0)
    y = h @ W_top3
    return y

_drawn_inputs = setup_inputs


def setup_inputs(seed=0):
    import zlib

    import numpy as np

    out = dict(_drawn_inputs(seed))
    spreads = {'b_top1': (0.0, 0.1), 'b_top2': (0.0, 0.1)}
    factors = {'tbl_0': 4.712,
     'tbl_1': 5.207,
     'tbl_2': 5.066,
     'tbl_3': 4.874,
     'tbl_4': 5.196,
     'tbl_5': 5.279,
     'tbl_6': 4.806,
     'tbl_7': 5.016,
     'tbl_8': 5.053,
     'tbl_9': 4.888,
     'tbl_10': 5.094,
     'tbl_11': 4.835,
     'tbl_12': 4.853,
     'tbl_13': 4.452,
     'tbl_14': 4.94,
     'tbl_15': 5.047,
     'tbl_16': 5.196,
     'tbl_17': 5.011,
     'tbl_18': 5.234,
     'tbl_19': 5.466,
     'tbl_20': 5.028,
     'tbl_21': 4.985,
     'tbl_22': 4.766,
     'tbl_23': 4.891,
     'tbl_24': 4.906,
     'tbl_25': 4.864,
     'tbl_26': 5.044,
     'tbl_27': 5.024,
     'tbl_28': 4.844,
     'tbl_29': 4.995,
     'tbl_30': 5.049,
     'tbl_31': 4.489,
     'tbl_32': 4.917,
     'tbl_33': 5.208,
     'tbl_34': 4.932,
     'tbl_35': 5.17,
     'tbl_36': 4.866,
     'tbl_37': 5.147,
     'tbl_38': 5.235,
     'L0_rec_W1': 5.357}
    for name, (base, spread) in spreads.items():
        noise = np.random.default_rng([zlib.crc32(name.encode()), seed]).standard_normal(out[name].shape)
        drawn = base * np.exp(spread * noise) if base else spread * noise
        out[name] = jnp.asarray(drawn.astype(out[name].dtype))
    for name, factor in factors.items():
        out[name] = (out[name] * factor).astype(out[name].dtype)
    return out
```

```python
from contextlib import ExitStack

import numpy as np
import concourse.bass as bass
import concourse.mybir as mybir

FIELDS, DIM, BATCH, OUT = 39, 16, 1024, 128
TILE = 128
TILES, PAIRS = BATCH // TILE, BATCH // TILE // 2
CHUNKS = 4
COLS = TILE * DIM // CHUNKS
OFFSETS = list(range(1, 20)) + [0]
SLOTS = [3] * 6 + [2]
STEPS = len(SLOTS)
ROWS = [s * FIELDS for s in SLOTS]
STACK = 3 * FIELDS
GROUP = 128 // DIM
GROUPS = 4
PART = 32
EXT = FIELDS + 1
PAIR = 2 * TILE
CTX, H1, H2 = 16, 512, 256
Z_RING = 4
TOP_AT = [(0, 1, 5), (0, 1, 6), (0, 2, 5), (0, 2, 6), (0, 3, 5), (0, 3, 6), (1, 0, 5)]
SPLIT_AT = [(2, 5), (2, 6), (3, 0), (3, 1)]


def build(nc, dense_t, ids, tables, w0_mn, w0_nm, w1, wt1, bt1, wt2, bt2, wt3,
          pick, ident, mask, out):
    f32, bf16, i32 = mybir.dt.float32, mybir.dt.bfloat16, mybir.dt.int32
    ALU, ACT = mybir.AluOpType, mybir.ActivationFunctionType

    with ExitStack() as ctx:
        def sbuf(name, shape, dt=f32):
            return ctx.enter_context(nc.sbuf_tensor(name, shape, dt))

        def sem(name):
            return ctx.enter_context(nc.semaphore(name))

        w0_sb = sbuf("w0_sb", [STACK, STEPS, OUT])
        w0_other = sbuf("w0_other", [STACK, STEPS, OUT])
        w1_sb = sbuf("w1_sb", [OUT, FIELDS, OUT])
        wt1_sb = sbuf("wt1_sb", [128, 2, H1])
        wt1_ctx = sbuf("wt1_ctx", [CTX, H1])
        wt2_sb = sbuf("wt2_sb", [128, H1 // 128, H2])
        wt3_sb = sbuf("wt3_sb", [128, H2 // 128])
        bt1_sb = sbuf("bt1_sb", [128, H1 // 128])
        bt2_sb = sbuf("bt2_sb", [128, H2 // 128])
        pick_in_sb = sbuf("pick_in_sb", [STACK, len(OFFSETS) * FIELDS + STACK])
        pick_all = sbuf("pick_all", [STACK, len(OFFSETS) * FIELDS + STACK], bf16)
        pick_sb = pick_all[:, 0:len(OFFSETS) * FIELDS]
        copies_sb = pick_all[:, len(OFFSETS) * FIELDS:]
        ident_sb = sbuf("ident_sb", [128, 128])
        ident_bf = sbuf("ident_bf", [128, 128], bf16)
        mask_sb = sbuf("mask_sb", [128, GROUP])
        ids_sb = sbuf("ids_sb", [TILE, TILES, FIELDS], i32)
        ids_now = sbuf("ids_now", [TILE, 2, FIELDS], i32)
        rows_sb = sbuf("rows_sb", [TILE, 2, FIELDS * DIM])
        parts_sb = sbuf("parts_sb", [TILE, DIM, STACK], bf16)
        rest_sb = sbuf("rest_sb", [TILE, DIM, FIELDS])
        gate_sb = sbuf("gate_sb", [1, 2])
        xt_sb = sbuf("xt_sb", [STACK, 2, TILE, DIM], bf16)
        a_sb = sbuf("a_sb", [STACK, 2, COLS])
        z_sb = sbuf("z_sb", [STACK, Z_RING, COLS])
        x1t_sb = sbuf("x1t_sb", [OUT, COLS])
        x1g_sb = sbuf("x1g_sb", [128, GROUPS, OUT])
        xd_sb = sbuf("xd_sb", [128, 2, GROUPS, GROUP, EXT])
        g_sb = sbuf("g_sb", [OUT, EXT, PAIR])
        z1_sb = sbuf("z1_sb", [OUT, PAIR])
        z2_sb = sbuf("z2_sb", [OUT, PAIR])
        ctx_sb = sbuf("ctx_sb", [CTX, PAIR])
        h1_sb = sbuf("h1_sb", [128, H1 // 128, PAIR])
        h2_sb = sbuf("h2_sb", [128, H2 // 128, PAIR])
        y_sb = sbuf("y_sb", [1, PAIRS, PAIR])

        ring = [ctx.enter_context(nc.psum_tensor(f"ring{k}", [128, COLS], f32)) for k in range(3)]
        acc = [ctx.enter_context(nc.psum_tensor(f"acc{k}", [128, COLS], f32)) for k in range(2)]
        turn = ctx.enter_context(nc.psum_tensor("turn", [128, COLS], f32))
        g_ps = ctx.enter_context(nc.psum_tensor("g_ps", [128, COLS], f32))
        top_ps = ctx.enter_context(nc.psum_tensor("top_ps", [128, COLS], f32))
        turn_bf = turn[:, :].bitcast(bf16)

        ids_in = sem("ids_in")
        pick_in = sem("pick_in")
        pick_ready = sem("pick_ready")
        w0_in = sem("w0_in")
        mask_in = sem("mask_in")
        top_in = sem("top_in")
        bias_in = sem("bias_in")
        ctx_in = sem("ctx_in")
        ident_bf_ready = sem("ident_bf_ready")
        w0_folded = sem("w0_folded")
        mask_set = sem("mask_set")
        ids_copied = sem("ids_copied")
        gate_passed = sem("gate_passed")
        gathered = [sem("gathered_even"), sem("gathered_odd")]
        split_step = sem("split_step")
        xt_turned = sem("xt_turned")
        xt_ready = sem("xt_ready")
        a_picked = sem("a_picked")
        a_ready = sem("a_ready")
        b_picked = sem("b_picked")
        z_ready = sem("z_ready")
        w0_done = sem("w0_done")
        x1t_ready = sem("x1t_ready")
        x1_turned = sem("x1_turned")
        x1g_ready = sem("x1g_ready")
        xg_picked = sem("xg_picked")
        xd_ready = sem("xd_ready")
        g_done = sem("g_done")
        g_ready = sem("g_ready")
        z1_ready = sem("z1_ready")
        top_done = sem("top_done")
        top_ready = sem("top_ready")
        stored = sem("stored")

        def wait(engine, semaphore, value):
            if isinstance(value, int) and value <= 0:
                return
            engine.wait_ge(semaphore, value)

        def by_pairs(engine, pair):
            pair(0, True, False)
            with engine.Fori(1, PAIRS - 1) as i:
                pair(i, False, False)
            pair(PAIRS - 1, False, True)

        block = ctx.enter_context(nc.Block())

        @block.sync
        def _(sp):
            full = STEPS - 1
            sp.dma_start(ids_sb[:, :, :], ids.rearrange("(t p) f -> p t f", p=TILE)).then_inc(ids_in, 16)
            sp.dma_start(ident_sb[:, :], ident).then_inc(mask_in, 16)
            sp.dma_start(mask_sb[:, :], mask).then_inc(mask_in, 16)
            sp.dma_start(pick_in_sb[:, :], pick).then_inc(pick_in, 16)
            for weights, dst in ((w0_mn, w0_sb), (w0_nm, w0_other)):
                sp.dma_start(dst[:, 0:full, :],
                             weights[0:full * STACK, :].rearrange("(t p) o -> p t o", p=STACK)).then_inc(w0_in, 16)
                left = weights.shape[0] - full * STACK
                sp.dma_start(dst[0:left, full, :], weights[full * STACK:, :]).then_inc(w0_in, 16)
            sp.dma_start(w1_sb[:, :, :], w1.rearrange("(m n) o -> n m o", n=OUT)).then_inc(top_in, 16)
            sp.dma_start(wt1_sb[:, :, :], wt1[0:2 * OUT, :].rearrange("(c p) h -> p c h", p=128)).then_inc(top_in, 16)
            sp.dma_start(wt1_ctx[:, :], wt1[2 * OUT:, :]).then_inc(top_in, 16)
            sp.dma_start(wt2_sb[:, :, :], wt2.rearrange("(c p) h -> p c h", p=128)).then_inc(top_in, 16)
            sp.dma_start(wt3_sb[:, :], wt3).then_inc(top_in, 16)
            sp.dma_start(bt1_sb[:, :], bt1).then_inc(bias_in, 16)
            sp.dma_start(bt2_sb[:, :], bt2).then_inc(bias_in, 16)

            def pair(j):
                wait(sp, top_done, 8 * j - 3)
                sp.dma_start(ctx_sb[:, :], dense_t[:, bass.ds(j * PAIR, PAIR)]).then_inc(ctx_in, 16)

            pair(0)
            with sp.Fori(1, PAIRS) as j:
                pair(j)
            sp.wait_ge(top_ready, 8 * PAIRS + 1)
            sp.dma_start(out, y_sb[:, :, :].rearrange("p j b -> p (j b)")).then_inc(stored, 16)
            sp.wait_ge(stored, 16)

        @block.gpsimd
        def _(pool):
            nc.gpsimd.memset(gate_sb[:, :], 0.0).then_inc(gate_passed, 1)
            pool.wait_ge(ids_in, 16)

            def pair(i, first, last):
                for u in range(2):
                    t = 2 * i + u
                    wait(pool, gathered[u], 16 * FIELDS * i)
                    nc.gpsimd.tensor_copy(ids_now[:, u, :], ids_sb[:, bass.ds(t, 1), :].rearrange(
                        "p t f -> p (t f)")).then_inc(ids_copied, 1)
                    pool.wait_ge(gate_passed, t + 1)
                    wait(pool, split_step, 4 * (t - 2) + 2)
                    pool.wait_ge(ids_copied, t + 1)
                    nc.gpsimd.tensor_tensor(gate_sb[:, 1:2], gate_sb[:, 0:1], gate_sb[:, 0:1],
                                            ALU.add).then_inc(gate_passed, 1)
                    for f in range(FIELDS):
                        nc.gpsimd.indirect_dma_start(
                            rows_sb[:, u, f * DIM:(f + 1) * DIM], None, tables[f],
                            bass.IndirectOffsetOnAxis(ap=ids_now[:, u, f:f + 1], axis=0)).then_inc(gathered[u], 16)

            by_pairs(pool, pair)

        @block.vector
        def _(dve):
            full = STEPS - 1
            dve.wait_ge(w0_in, 64)
            nc.vector.tensor_tensor(w0_sb[:, 0:full, :], w0_sb[:, 0:full, :], w0_other[:, 0:full, :],
                                    ALU.add).then_inc(w0_folded, 1)
            nc.vector.tensor_tensor(w0_sb[0:FIELDS, full, :], w0_sb[0:FIELDS, full, :],
                                    w0_other[0:FIELDS, full, :], ALU.add).then_inc(w0_folded, 1)
            dve.wait_ge(mask_in, 32)
            nc.vector.tensor_copy(ident_bf[:, :], ident_sb[:, :]).then_inc(ident_bf_ready, 1)
            dve.wait_ge(pick_in, 16)
            nc.vector.tensor_copy(pick_all[:, :], pick_in_sb[:, :]).then_inc(pick_ready, 1)
            for half in range(2):
                for g in range(GROUPS):
                    nc.vector.tensor_copy(xd_sb[:, half, g, :, FIELDS], mask_sb[:, :]).then_inc(mask_set, 1)

            def split(t, u, step):
                rows = rows_sb[:, u, :].rearrange("p (m d) -> p d m", d=DIM)
                part = [parts_sb[:, :, k * FIELDS:(k + 1) * FIELDS] for k in range(3)]
                if step == 0:
                    dve.wait_ge(gathered[u], 8 * FIELDS * (t - u + 2))
                    wait(dve, xt_turned, 2 * t)
                    nc.vector.tensor_copy(part[0], rows).then_inc(split_step, 1)
                    return
                dve.wait_ge(split_step, 4 * t + step)
                if step == 1:
                    nc.vector.tensor_tensor(rest_sb[:, :, :], rows, part[0], ALU.subtract).then_inc(split_step, 1)
                elif step == 2:
                    nc.vector.tensor_copy(part[1], rest_sb[:, :, :]).then_inc(split_step, 1)
                else:
                    nc.vector.tensor_tensor(part[2], rest_sb[:, :, :], part[1], ALU.subtract).then_inc(split_step, 1)

            def product(c, q, s):
                rows, slot = ROWS[s], (q * STEPS + s) % Z_RING
                if s == 0:
                    dve.wait_ge(a_ready, c + 1)
                dve.wait_ge(b_picked, STEPS * c + s + 1)
                wait(dve, w0_done, STEPS * c + s - Z_RING + 1)
                where = ring[(0, 1, 2, 0, 1, 0, 1)[s]]
                nc.vector.tensor_tensor(z_sb[0:rows, slot, :], where[0:rows, :], a_sb[0:rows, q % 2, :],
                                        ALU.mult).then_inc(z_ready, 1)

            def diagonal(c, q):
                for half in range(2):
                    if half == 0:
                        dve.wait_ge(xg_picked, c + 1)
                        wait(dve, g_done, GROUPS * (c - 1))
                    g0, shape = 2 * half, [128, 2, GROUP, FIELDS]
                    x = ring[2][:, g0 * FIELDS:(g0 + 2) * FIELDS].rearrange("p (g m) -> p g m", g=2)
                    nc.vector.tensor_tensor(
                        xd_sb[:, q % 2, g0:g0 + 2, :, 0:FIELDS], x.unsqueeze(2).to_broadcast(shape),
                        mask_sb[:, :].unsqueeze(1).unsqueeze(3).to_broadcast(shape), ALU.mult).then_inc(xd_ready, 1)

            def chunk(t, u, q, first_tile, last_tile):
                c = CHUNKS * t + q
                for s in range(STEPS):
                    product(c, q, s)
                    if s == 4:
                        diagonal(c, q)
                    if (q, s) in SPLIT_AT and not (first_tile or last_tile):
                        split(t + 1, 1 - u, SPLIT_AT.index((q, s)))
                if q == 3 and first_tile:
                    for step in range(4):
                        split(t + 1, 1 - u, step)

            def copy_sum_x1(j):
                dve.wait_ge(g_ready, 8 * GROUPS * (j + 1))
                dve.wait_ge(top_ready, 8 * j + 1)
                nc.vector.tensor_copy(z1_sb[:, :], g_sb[:, FIELDS, :]).then_inc(z1_ready, 1)

            def pair(i, first, last):
                for u in range(2):
                    for q in range(CHUNKS):
                        chunk(2 * i + u, u, q, first and u == 0, last and u == 1)
                        if (u, q) == (0, 0) and not first:
                            copy_sum_x1(i - 1)

            for step in range(4):
                split(0, 0, step)
            by_pairs(dve, pair)
            copy_sum_x1(PAIRS - 1)

        @block.scalar
        def _(act):
            act.wait_ge(bias_in, 32)
            nc.scalar.copy(y_sb[:, 0, 0:1], bt1_sb[0:1, 0:1]).then_inc(top_ready, 1)

            def keep_xt(t, u, half):
                act.wait_ge(xt_turned, 2 * t + half + 1)
                if half == 0:
                    wait(act, xg_picked, CHUNKS * (t - 1))
                nc.scalar.copy(xt_sb[:, u, :, 8 * half:8 * half + 8],
                               turn_bf[0:STACK, :].rearrange("k (d b) -> k b d", d=8)).then_inc(xt_ready, 1)

            def keep_a(c, q):
                act.wait_ge(a_picked, c + 1)
                wait(act, z_ready, STEPS * (c - 1))
                nc.scalar.copy(a_sb[:, q % 2, :], ring[2][0:STACK, :]).then_inc(a_ready, 1)

            def keep_x1t(c, q):
                act.wait_ge(w0_done, STEPS * (c + 1))
                wait(act, x1_turned, c)
                nc.scalar.copy(x1t_sb[:, :], acc[q % 2][:, :]).then_inc(x1t_ready, 1)

            def keep_x1g(c):
                act.wait_ge(x1_turned, c + 1)
                wait(act, g_done, GROUPS * c)
                nc.scalar.copy(x1g_sb[:, :, :], turn[:, :].rearrange("p (g n) -> p g n", g=GROUPS)
                               ).then_inc(x1g_ready, 1)

            def keep_g(i, u, q, g):
                act.wait_ge(g_done, GROUPS * (CHUNKS * (2 * i + u) + q) + g + 1)
                if (u, q, g) == (0, 0, 0):
                    wait(act, top_done, 8 * i - 7)
                    wait(act, z1_ready, i)
                b0 = u * TILE + (q * GROUPS + g) * GROUP
                nc.scalar.copy(g_sb[:, :, b0:b0 + GROUP].rearrange("n m b -> n b m"),
                               g_ps[:, 0:GROUP * EXT].rearrange("n (b m) -> n b m", m=EXT)).then_inc(g_ready, 1)

            def keep_top(j, k):
                act.wait_ge(top_done, 8 * j + k + 1)
                if k == 0:
                    nc.scalar.copy(z2_sb[:, :], top_ps[:, 0:PAIR]).then_inc(top_ready, 1)
                elif k < 5:
                    nc.scalar.activation(h1_sb[:, k - 1, :], top_ps[:, 0:PAIR], ACT.Relu,
                                         bias=bt1_sb[:, k - 1:k]).then_inc(top_ready, 1)
                elif k < 7:
                    nc.scalar.activation(h2_sb[:, k - 5, :], top_ps[:, 0:PAIR], ACT.Relu,
                                         bias=bt2_sb[:, k - 5:k - 4]).then_inc(top_ready, 1)
                else:
                    nc.scalar.copy(y_sb[:, bass.ds(j, 1), :].rearrange("p j b -> p (j b)"),
                                   top_ps[0:1, 0:PAIR]).then_inc(top_ready, 1)

            def chunk(i, u, q, first, last):
                t = 2 * i + u
                c = CHUNKS * t + q
                first_tile, last_tile = first and u == 0, last and u == 1
                turns_xt = q == 3 and not (first_tile or last_tile)
                before = (i, u, q - 1) if q else (i, 0, 3) if u else (i - 1, 1, 3)
                has_before = not (first_tile and q == 0)
                if has_before:
                    keep_x1g(c - 1)
                    keep_g(*before, 0)
                if turns_xt:
                    keep_xt(t + 1, 1 - u, 0)
                if has_before:
                    keep_g(*before, 1)
                    keep_g(*before, 2)
                if turns_xt:
                    keep_xt(t + 1, 1 - u, 1)
                if not (q == 3 and (first_tile or last_tile)):
                    keep_a(c + 1, (q + 1) % 4)
                if has_before:
                    keep_g(*before, 3)
                if (u, q, 5) in TOP_AT and not first:
                    keep_top(i - 1, TOP_AT.index((u, q, 5)) + 1)
                keep_x1t(c, q)
                if (u, q, 6) in TOP_AT and not first:
                    keep_top(i - 1, TOP_AT.index((u, q, 6)) + 1)
                if q == 3 and first_tile:
                    keep_xt(t + 1, 1 - u, 0)
                    keep_xt(t + 1, 1 - u, 1)
                    keep_a(c + 1, 0)

            def pair(i, first, last):
                for u in range(2):
                    for q in range(CHUNKS):
                        chunk(i, u, q, first, last)
                        if (u, q) == (0, 0) and not first:
                            keep_top(i - 1, 0)

            keep_xt(0, 0, 0)
            keep_xt(0, 0, 1)
            keep_a(0, 0)
            by_pairs(act, pair)
            keep_x1g(CHUNKS * TILES - 1)
            for g in range(GROUPS):
                keep_g(PAIRS - 1, 1, 3, g)
            for k in range(8):
                keep_top(PAIRS - 1, k)

        @block.tensor
        def _(pe):
            def turn_xt(t, half):
                if half == 0:
                    pe.wait_ge(split_step, 4 * t + 4)
                    wait(pe, x1g_ready, 4 * t - 1)
                else:
                    pe.wait_ge(xt_ready, 2 * t + 1)
                for d in range(8):
                    last = nc.tensor.transpose(turn_bf[0:STACK, d * TILE:(d + 1) * TILE],
                                               parts_sb[:, 8 * half + d, :], ident_bf[:, :])
                last.then_inc(xt_turned, 1)

            def chunk_of_x(u, q):
                return xt_sb[:, u, PART * q:PART * (q + 1), :].rearrange("k b d -> k (b d)")

            def pick_a(u, q):
                nc.tensor.matmul(ring[2][0:STACK, :], copies_sb, chunk_of_x(u, q),
                                 start=True, stop=True).then_inc(a_picked, 1)

            def pick_b(u, q, s):
                k0 = sum(ROWS[:s])
                nc.tensor.matmul(ring[(0, 1, 2, 0, 1, 0, 1)[s]][0:ROWS[s], :], pick_sb[:, k0:k0 + ROWS[s]],
                                 chunk_of_x(u, q), start=True, stop=True).then_inc(b_picked, 1)

            def weigh(c, q, s):
                pe.wait_ge(z_ready, STEPS * c + s + 1)
                if s == 0:
                    wait(pe, x1t_ready, c - 1)
                nc.tensor.matmul(acc[q % 2][:, :], w0_sb[0:ROWS[s], s, :], z_sb[0:ROWS[s], (q * STEPS + s) % Z_RING, :],
                                 start=(s == 0), stop=(s == STEPS - 1)).then_inc(w0_done, 1)

            def pick_x(u, q):
                for g in range(GROUPS):
                    b0 = (q * GROUPS + g) * GROUP
                    last = nc.tensor.matmul(ring[2][:, g * FIELDS:(g + 1) * FIELDS],
                                            xt_sb[:, u, b0:b0 + GROUP, :].rearrange("k b d -> k (b d)"),
                                            pick_sb[:, (len(OFFSETS) - 1) * FIELDS:], start=True, stop=True)
                last.then_inc(xg_picked, 1)

            def turn_x1(c, q, xt_halves):
                pe.wait_ge(x1t_ready, c + 1)
                if q == 3:
                    wait(pe, xt_ready, xt_halves)
                else:
                    wait(pe, x1g_ready, c)
                for g in range(GROUPS):
                    last = nc.tensor.transpose(turn[:, g * OUT:(g + 1) * OUT],
                                               x1t_sb[:, g * 128:(g + 1) * 128], ident_sb[:, :])
                last.then_inc(x1_turned, 1)

            def g_group(c, q, g):
                if g == 0:
                    pe.wait_ge(x1g_ready, c + 1)
                if g % 2 == 0:
                    pe.wait_ge(xd_ready, 2 * c + g // 2 + 1)
                wait(pe, g_ready, GROUPS * c + g)
                nc.tensor.matmul(g_ps[:, 0:GROUP * EXT], x1g_sb[:, g, :],
                                 xd_sb[:, q % 2, g, :, :].rearrange("p b m -> p (b m)"),
                                 start=True, stop=True).then_inc(g_done, 1)

            def top(j, k):
                pe.wait_ge(top_ready, 8 * j + k + 1)
                dst = top_ps[:, 0:PAIR]
                if k == 0:
                    pe.wait_ge(g_ready, 8 * GROUPS * (j + 1))
                    terms = [(w1_sb[:, m, :], g_sb[:, m, :]) for m in range(FIELDS)]
                elif k < 5:
                    if k == 1:
                        pe.wait_ge(z1_ready, j + 1)
                        pe.wait_ge(ctx_in, 16 * (j + 1))
                    h = slice((k - 1) * 128, k * 128)
                    terms = [(wt1_sb[:, 0, h], z1_sb[:, :]), (wt1_sb[:, 1, h], z2_sb[:, :]), (wt1_ctx[:, h], ctx_sb[:, :])]
                elif k < 7:
                    h = slice((k - 5) * 128, (k - 4) * 128)
                    terms = [(wt2_sb[:, n, h], h1_sb[:, n, :]) for n in range(H1 // 128)]
                else:
                    dst = top_ps[0:1, 0:PAIR]
                    terms = [(wt3_sb[:, n:n + 1], h2_sb[:, n, :]) for n in range(H2 // 128)]
                for n, (w, x) in enumerate(terms):
                    last = nc.tensor.matmul(dst, w, x, start=(n == 0), stop=(n == len(terms) - 1))
                last.then_inc(top_done, 1)

            def chunk(i, u, q, first, last):
                t = 2 * i + u
                c = CHUNKS * t + q
                first_tile, last_tile = first and u == 0, last and u == 1
                nxt_u, nxt_q = (u, q + 1) if q < 3 else (1 - u, 0)
                alone = q == 3 and (first_tile or last_tile)
                has_before = not (first_tile and q == 0)
                for s in range(STEPS):
                    if s == 0:
                        pe.wait_ge(a_ready, c + 1)
                        pick_b(u, q, 2)
                    elif s == 1:
                        pe.wait_ge(z_ready, STEPS * c + 1)
                        pick_b(u, q, 3)
                    elif s == 2:
                        pe.wait_ge(z_ready, STEPS * c + 2)
                        pick_b(u, q, 4)
                        pe.wait_ge(z_ready, STEPS * c + 3)
                        pick_x(u, q)
                    elif s == 3:
                        pe.wait_ge(z_ready, STEPS * c + 4)
                        pick_b(u, q, 5)
                    elif s == 4:
                        pe.wait_ge(z_ready, STEPS * c + 5)
                        pick_b(u, q, 6)
                    elif s == 5 and not alone:
                        pe.wait_ge(xd_ready, 2 * (c + 1))
                        if q == 3:
                            pe.wait_ge(xt_ready, 2 * t + 4)
                        pick_a(nxt_u, nxt_q)
                    elif s == 6 and not alone:
                        pe.wait_ge(z_ready, STEPS * c + 6)
                        pick_b(nxt_u, nxt_q, 0)
                        pe.wait_ge(z_ready, STEPS * c + 7)
                        pick_b(nxt_u, nxt_q, 1)
                    weigh(c, q, s)
                    if has_before and s == 1:
                        turn_x1(c - 1, (q - 1) % 4, 2 * t + 2)
                    if has_before and s >= 2 and s < 6:
                        g_group(c - 1, (q - 1) % 4, s - 2)
                    if q == 3 and not alone and s in (2, 4):
                        turn_xt(t + 1, s // 2 - 1)
                    if (u, q, s) in TOP_AT and not first:
                        top(i - 1, TOP_AT.index((u, q, s)) + 1)
                if q == 3 and first_tile:
                    turn_xt(t + 1, 0)
                    turn_xt(t + 1, 1)
                    begin(t + 1, nxt_u)

            def begin(t, u):
                pe.wait_ge(xt_ready, 2 * t + 2)
                wait(pe, xd_ready, 2 * CHUNKS * t)
                pick_a(u, 0)
                wait(pe, z_ready, STEPS * CHUNKS * t)
                pick_b(u, 0, 0)
                pick_b(u, 0, 1)

            def pair(i, first, last):
                for u in range(2):
                    for q in range(CHUNKS):
                        chunk(i, u, q, first, last)
                        if (u, q) == (0, 0) and not first:
                            top(i - 1, 0)

            pe.wait_ge(ident_bf_ready, 1)
            turn_xt(0, 0)
            turn_xt(0, 1)
            pe.wait_ge(pick_ready, 1)
            pe.wait_ge(w0_folded, 2)
            pe.wait_ge(mask_set, 2 * GROUPS)
            pe.wait_ge(top_in, 80)
            begin(0, 0)
            by_pairs(pe, pair)
            turn_x1(CHUNKS * TILES - 1, 3, 0)
            for g in range(GROUPS):
                g_group(CHUNKS * TILES - 1, 3, g)
            for k in range(8):
                top(PAIRS - 1, k)


def _constants():
    pick = np.zeros((3, FIELDS, len(OFFSETS), FIELDS), np.float32)
    for n, k in enumerate(OFFSETS):
        for m in range(FIELDS):
            pick[:, (m + k) % FIELDS, n, m] = 1
    copies = np.zeros((3, FIELDS, 3, FIELDS), np.float32)
    for m in range(FIELDS):
        copies[:, m, :, m] = 1
    mask = np.zeros((GROUP, DIM, GROUP), np.float32)
    for b in range(GROUP):
        mask[b, :, b] = 1
    return {"pick": np.concatenate([pick.reshape(STACK, -1), copies.reshape(STACK, -1)], 1),
            "ident": np.eye(128, dtype=np.float32), "mask": mask.reshape(128, GROUP)}


def kernel(**inputs):
    import concourse.bacc as _bacc
    from concourse.bass_utils import run_bass_kernel_spmd as _run

    nc = _bacc.Bacc("TRN2", target_bir_lowering=False, num_devices=1)
    w0 = np.asarray(inputs["L0_rec_W0"]).reshape(FIELDS, FIELDS, OUT)
    m = np.arange(FIELDS)
    arrays = {
        "in_dense_t": np.ascontiguousarray(np.asarray(inputs["dense_ctx"]).T),
        "in_ids": np.asarray(inputs["ids"]),
        "in_w0_mn": np.concatenate([w0[m, (m + k) % FIELDS] for k in OFFSETS]),
        "in_w0_nm": np.concatenate([w0[(m + k) % FIELDS, m] for k in OFFSETS if k]),
        "in_w1": np.asarray(inputs["L0_rec_W1"]),
        "in_wt1": np.asarray(inputs["W_top1"]), "in_bt1": np.asarray(inputs["b_top1"]).reshape(-1, 128).T,
        "in_wt2": np.asarray(inputs["W_top2"]), "in_bt2": np.asarray(inputs["b_top2"]).reshape(-1, 128).T,
        "in_wt3": np.asarray(inputs["W_top3"]).reshape(-1, 128).T,
    }
    arrays.update({f"in_{n}": a for n, a in _constants().items()})
    arrays.update({f"in_tbl_{f}": np.asarray(inputs[f"tbl_{f}"]) for f in range(FIELDS)})
    arrays = {n: np.ascontiguousarray(a) for n, a in arrays.items()}
    ap = {n[3:]: nc.dram_tensor(n, a.shape, mybir.dt.from_np(a.dtype), kind="ExternalInput").ap()
          for n, a in arrays.items()}
    out = nc.dram_tensor("out_y", (1, BATCH), mybir.dt.float32, kind="ExternalOutput").ap()
    build(nc, ap["dense_t"], ap["ids"], [ap[f"tbl_{f}"] for f in range(FIELDS)], ap["w0_mn"], ap["w0_nm"],
          ap["w1"], ap["wt1"], ap["bt1"], ap["wt2"], ap["bt2"], ap["wt3"],
          ap["pick"], ap["ident"], ap["mask"], out)
    r = _run(nc, [arrays], core_ids=[0])
    return np.asarray(r.results[0]["out_y"]).reshape(BATCH, 1)
```

```python
from contextlib import ExitStack

import numpy as np
import concourse.bass as bass
import concourse.mybir as mybir

FIELDS, DIM, BATCH, OUT = 39, 16, 1024, 128
TILE = 128
TILES, PAIRS = BATCH // TILE, BATCH // TILE // 2
CHUNKS = 4
COLS = TILE * DIM // CHUNKS
OFFSETS = list(range(1, 20)) + [0]
SLOTS = [3] * 6 + [2]
STEPS = len(SLOTS)
ROWS = [s * FIELDS for s in SLOTS]
STACK = 3 * FIELDS
GROUP = 128 // DIM
GROUPS = 4
PART = 32
EXT = FIELDS + 1
CTX, H1, H2 = 16, 512, 256
Z_RING = 4
SUM_AT = {(1, 2): 2, (1, 3): 2, (1, 4): 2, (1, 5): 3, (1, 6): 4,
          (2, 0): 3, (2, 1): 2, (2, 2): 1, (2, 3): 2, (2, 4): 2, (2, 5): 2, (2, 6): 3,
          (3, 0): 3, (3, 1): 3, (3, 2): 2, (3, 3): 2, (3, 4): 1}
SUM_END = (3, 4)
H1_AT = [(3, 6), (0, 0), (0, 1), (0, 2)]
H2_AT = [(0, 4), (0, 5)]
Y_AT = (1, 0)
SPLIT_AT = [[(2, 4), (2, 6), (3, 0), (3, 0)], [(2, 3), (2, 4), (2, 5), (2, 5)], [(1, 2), (1, 4), (1, 6), (2, 0)]]
TURN_AT = [[(3, 1), (3, 2)], [(2, 5), (2, 6)], [(2, 1), (2, 2)]]


def build(nc, ctx_t, ids, tables, w0_mn, w0_nm, w1, wt1, wt1_rest, wt2, bt2, wt3,
          pick, ident, mask, out):
    f32, f32r, bf16, i32 = mybir.dt.float32, mybir.dt.float32r, mybir.dt.bfloat16, mybir.dt.int32
    ALU, ACT = mybir.AluOpType, mybir.ActivationFunctionType

    with ExitStack() as ctx:
        def sbuf(name, shape, dt=f32):
            return ctx.enter_context(nc.sbuf_tensor(name, shape, dt))

        def sem(name):
            return ctx.enter_context(nc.semaphore(name))

        w0_sb = sbuf("w0_sb", [STACK, STEPS, OUT])
        w0_other = sbuf("w0_other", [STACK, STEPS, OUT])
        w0_hi = sbuf("w0_hi", [STACK, STEPS, OUT], f32r)
        w0_lo = sbuf("w0_lo", [STACK, STEPS, OUT], f32r)
        w1_sb = sbuf("w1_sb", [OUT, FIELDS, OUT])
        wt1_sb = sbuf("wt1_sb", [128, 2, H1])
        wt1_ctx = sbuf("wt1_ctx", [CTX + 1, H1])
        wt2_sb = sbuf("wt2_sb", [128, H1 // 128, H2])
        wt3_sb = sbuf("wt3_sb", [128, H2 // 128])
        bt2_sb = sbuf("bt2_sb", [128, H2 // 128])
        pick_in_sb = sbuf("pick_in_sb", [STACK, len(OFFSETS) * FIELDS + STACK])
        pick_all = sbuf("pick_all", [STACK, len(OFFSETS) * FIELDS + STACK], bf16)
        pick_sb = pick_all[:, 0:len(OFFSETS) * FIELDS]
        copies_sb = pick_all[:, len(OFFSETS) * FIELDS:]
        ident_sb = sbuf("ident_sb", [128, 128])
        ident_bf = sbuf("ident_bf", [128, 128], bf16)
        mask_sb = sbuf("mask_sb", [128, GROUP])
        ids_sb = sbuf("ids_sb", [TILE, TILES, FIELDS], i32)
        ids_now = sbuf("ids_now", [TILE, 2, FIELDS], i32)
        rows_sb = sbuf("rows_sb", [TILE, 2, FIELDS * DIM])
        parts_sb = sbuf("parts_sb", [TILE, DIM, STACK], bf16)
        rest_sb = sbuf("rest_sb", [TILE, DIM, FIELDS])
        gate_sb = sbuf("gate_sb", [1, 2])
        xt_sb = sbuf("xt_sb", [STACK, 2, TILE, DIM], bf16)
        a_sb = sbuf("a_sb", [STACK, 2, COLS])
        z_sb = sbuf("z_sb", [STACK, Z_RING, COLS])
        z_hi = sbuf("z_hi", [STACK, Z_RING, COLS], f32r)
        z_lo = sbuf("z_lo", [STACK, Z_RING, COLS], f32r)
        x1t_sb = sbuf("x1t_sb", [OUT, COLS])
        x1g_sb = sbuf("x1g_sb", [128, GROUPS, OUT])
        xd_sb = sbuf("xd_sb", [128, 2, GROUPS, GROUP, EXT])
        g_sb = sbuf("g_sb", [OUT, 2, EXT, TILE])
        z2_sb = sbuf("z2_sb", [OUT, TILE])
        ctx_sb = sbuf("ctx_sb", [CTX + 1, BATCH])
        h1_sb = sbuf("h1_sb", [128, H1 // 128, TILE])
        h2_sb = sbuf("h2_sb", [128, H2 // 128, TILE])
        y_sb = sbuf("y_sb", [1, TILES, TILE])

        ring = [ctx.enter_context(nc.psum_tensor(f"ring{k}", [128, COLS], f32)) for k in range(3)]
        acc = [ctx.enter_context(nc.psum_tensor(f"acc{k}", [128, COLS], f32)) for k in range(2)]
        turn = ctx.enter_context(nc.psum_tensor("turn", [128, COLS], f32))
        g_ps = ctx.enter_context(nc.psum_tensor("g_ps", [128, COLS], f32))
        top_ps = ctx.enter_context(nc.psum_tensor("top_ps", [128, COLS], f32))
        turn_bf = turn[:, :].bitcast(bf16)

        ids_in = sem("ids_in")
        pick_in = sem("pick_in")
        pick_ready = sem("pick_ready")
        w0_in = sem("w0_in")
        mask_in = sem("mask_in")
        top_in = sem("top_in")
        bias_in = sem("bias_in")
        ident_bf_ready = sem("ident_bf_ready")
        w0_folded = sem("w0_folded")
        mask_set = sem("mask_set")
        ids_copied = sem("ids_copied")
        gate_passed = sem("gate_passed")
        gathered = [sem("gathered_even"), sem("gathered_odd")]
        split_step = sem("split_step")
        xt_turned = sem("xt_turned")
        xt_ready = sem("xt_ready")
        a_picked = sem("a_picked")
        a_ready = sem("a_ready")
        b_picked = sem("b_picked")
        z_ready = sem("z_ready")
        zh_ready = sem("zh_ready")
        zl_ready = sem("zl_ready")
        w0_done = sem("w0_done")
        x1t_ready = sem("x1t_ready")
        x1_turned = sem("x1_turned")
        x1g_ready = sem("x1g_ready")
        xg_picked = sem("xg_picked")
        xd_ready = sem("xd_ready")
        g_done = sem("g_done")
        g_ready = sem("g_ready")
        top_done = sem("top_done")
        top_ready = sem("top_ready")
        stored = sem("stored")

        def wait(engine, semaphore, value):
            if isinstance(value, int) and value <= 0:
                return
            engine.wait_ge(semaphore, value)

        def kind(first, u):
            return u if first else 2

        def late_a(first, u, q):
            return first and u == 0 and q == 3

        def by_pairs(engine, pair):
            pair(0, True, False)
            with engine.Fori(1, PAIRS - 1) as i:
                pair(i, False, False)
            pair(PAIRS - 1, False, True)

        block = ctx.enter_context(nc.Block())

        @block.sync
        def _(sp):
            full = STEPS - 1
            sp.dma_start(ids_sb[:, :, :], ids.rearrange("(t p) f -> p t f", p=TILE)).then_inc(ids_in, 16)
            sp.dma_start(ident_sb[:, :], ident).then_inc(mask_in, 16)
            sp.dma_start(mask_sb[:, :], mask).then_inc(mask_in, 16)
            sp.dma_start(pick_in_sb[:, :], pick).then_inc(pick_in, 16)
            for weights, dst in ((w0_mn, w0_sb), (w0_nm, w0_other)):
                sp.dma_start(dst[:, 0:full, :],
                             weights[0:full * STACK, :].rearrange("(t p) o -> p t o", p=STACK)).then_inc(w0_in, 16)
                left = weights.shape[0] - full * STACK
                sp.dma_start(dst[0:left, full, :], weights[full * STACK:, :]).then_inc(w0_in, 16)
            sp.dma_start(w1_sb[:, :, :], w1.rearrange("(m n) o -> n m o", n=OUT)).then_inc(top_in, 16)
            sp.dma_start(wt1_sb[:, :, :], wt1.rearrange("(c p) h -> p c h", p=128)).then_inc(top_in, 16)
            sp.dma_start(wt1_ctx[:, :], wt1_rest).then_inc(top_in, 16)
            sp.dma_start(wt2_sb[:, :, :], wt2.rearrange("(c p) h -> p c h", p=128)).then_inc(top_in, 16)
            sp.dma_start(wt3_sb[:, :], wt3).then_inc(top_in, 16)
            sp.dma_start(bt2_sb[:, :], bt2).then_inc(bias_in, 16)
            sp.dma_start(ctx_sb[:, :], ctx_t).then_inc(top_in, 16)
            sp.wait_ge(top_ready, 5 * TILES + 1)
            sp.dma_start(out, y_sb[:, :, :].rearrange("p j b -> p (j b)")).then_inc(stored, 16)
            sp.wait_ge(stored, 16)

        @block.gpsimd
        def _(pool):
            nc.gpsimd.memset(gate_sb[:, :], 0.0).then_inc(gate_passed, 1)
            pool.wait_ge(ids_in, 16)

            def pair(i, first, last):
                for u in range(2):
                    t = 2 * i + u
                    wait(pool, gathered[u], 16 * FIELDS * i)
                    nc.gpsimd.tensor_copy(ids_now[:, u, :], ids_sb[:, bass.ds(t, 1), :].rearrange(
                        "p t f -> p (t f)")).then_inc(ids_copied, 1)
                    pool.wait_ge(gate_passed, t + 1)
                    wait(pool, split_step, 4 * (t - 2) + 2)
                    pool.wait_ge(ids_copied, t + 1)
                    nc.gpsimd.tensor_tensor(gate_sb[:, 1:2], gate_sb[:, 0:1], gate_sb[:, 0:1],
                                            ALU.add).then_inc(gate_passed, 1)
                    for f in range(FIELDS):
                        nc.gpsimd.indirect_dma_start(
                            rows_sb[:, u, f * DIM:(f + 1) * DIM], None, tables[f],
                            bass.IndirectOffsetOnAxis(ap=ids_now[:, u, f:f + 1], axis=0)).then_inc(gathered[u], 16)

            by_pairs(pool, pair)

        @block.vector
        def _(dve):
            full = STEPS - 1
            dve.wait_ge(w0_in, 64)
            nc.vector.tensor_tensor(w0_sb[:, 0:full, :], w0_sb[:, 0:full, :], w0_other[:, 0:full, :],
                                    ALU.add).then_inc(w0_folded, 1)
            nc.vector.tensor_tensor(w0_sb[0:FIELDS, full, :], w0_sb[0:FIELDS, full, :],
                                    w0_other[0:FIELDS, full, :], ALU.add).then_inc(w0_folded, 1)
            dve.wait_ge(w0_folded, 2)
            nc.vector.tensor_copy(w0_hi[:, 0:full, :], w0_sb[:, 0:full, :]).then_inc(w0_folded, 1)
            nc.vector.tensor_copy(w0_hi[0:ROWS[full], full, :], w0_sb[0:ROWS[full], full, :]).then_inc(w0_folded, 1)
            dve.wait_ge(w0_folded, 4)
            nc.vector.tensor_tensor(w0_lo[:, 0:full, :], w0_sb[:, 0:full, :], w0_hi[:, 0:full, :].bitcast(f32),
                                    ALU.subtract).then_inc(w0_folded, 1)
            nc.vector.tensor_tensor(w0_lo[0:ROWS[full], full, :], w0_sb[0:ROWS[full], full, :],
                                    w0_hi[0:ROWS[full], full, :].bitcast(f32), ALU.subtract).then_inc(w0_folded, 1)
            dve.wait_ge(mask_in, 32)
            nc.vector.tensor_copy(ident_bf[:, :], ident_sb[:, :]).then_inc(ident_bf_ready, 1)
            dve.wait_ge(pick_in, 16)
            nc.vector.tensor_copy(pick_all[:, :], pick_in_sb[:, :]).then_inc(pick_ready, 1)
            for half in range(2):
                for g in range(GROUPS):
                    nc.vector.tensor_copy(xd_sb[:, half, g, :, FIELDS], mask_sb[:, :]).then_inc(mask_set, 1)

            def split(t, u, step):
                rows = rows_sb[:, u, :].rearrange("p (m d) -> p d m", d=DIM)
                part = [parts_sb[:, :, k * FIELDS:(k + 1) * FIELDS] for k in range(3)]
                if step == 0:
                    dve.wait_ge(gathered[u], 8 * FIELDS * (t - u + 2))
                    wait(dve, xt_turned, 2 * t)
                    nc.vector.tensor_copy(part[0], rows).then_inc(split_step, 1)
                    return
                dve.wait_ge(split_step, 4 * t + step)
                if step == 1:
                    nc.vector.tensor_tensor(rest_sb[:, :, :], rows, part[0], ALU.subtract).then_inc(split_step, 1)
                elif step == 2:
                    nc.vector.tensor_copy(part[1], rest_sb[:, :, :]).then_inc(split_step, 1)
                else:
                    nc.vector.tensor_tensor(part[2], rest_sb[:, :, :], part[1], ALU.subtract).then_inc(split_step, 1)

            def product(c, q, s):
                rows, slot = ROWS[s], (q * STEPS + s) % Z_RING
                if s == 0:
                    dve.wait_ge(a_ready, c + 1)
                dve.wait_ge(b_picked, STEPS * c + s + 1)
                wait(dve, zl_ready, STEPS * c + s - Z_RING + 1)
                where = ring[(0, 1, 2, 0, 1, 0, 1)[s]]
                nc.vector.tensor_tensor(z_sb[0:rows, slot, :], where[0:rows, :], a_sb[0:rows, q % 2, :],
                                        ALU.mult).then_inc(z_ready, 1)

            def rest(c, q, s):
                rows, slot = ROWS[s], (q * STEPS + s) % Z_RING
                dve.wait_ge(zh_ready, STEPS * c + s + 1)
                wait(dve, w0_done, STEPS * c + s - Z_RING + 1)
                nc.vector.tensor_tensor(z_lo[0:rows, slot, :], z_sb[0:rows, slot, :],
                                        z_hi[0:rows, slot, :].bitcast(f32), ALU.subtract).then_inc(zl_ready, 1)

            def diagonal(c, q, half):
                if half == 0:
                    dve.wait_ge(xg_picked, c + 1)
                    wait(dve, g_done, GROUPS * (c - 1))
                g0, shape = 2 * half, [128, 2, GROUP, FIELDS]
                x = ring[2][:, g0 * FIELDS:(g0 + 2) * FIELDS].rearrange("p (g m) -> p g m", g=2)
                nc.vector.tensor_tensor(
                    xd_sb[:, q % 2, g0:g0 + 2, :, 0:FIELDS], x.unsqueeze(2).to_broadcast(shape),
                    mask_sb[:, :].unsqueeze(1).unsqueeze(3).to_broadcast(shape), ALU.mult).then_inc(xd_ready, 1)

            def chunk(t, u, q, first, last_tile, carried):
                c = CHUNKS * t + q
                for s in range(STEPS):
                    product(c, q, s)
                    if s >= 2:
                        rest(c, q, s - 2)
                    elif carried:
                        rest(c - 1, (q - 1) % CHUNKS, s + 5)
                    if late_a(first, u, q):
                        if s in (4, 5):
                            diagonal(c, q, s - 4)
                    elif s == 6:
                        diagonal(c, q, 0)
                    if s == 0 and carried and not late_a(first, 1 - u, (q - 1) % CHUNKS):
                        diagonal(c - 1, (q - 1) % CHUNKS, 1)
                    for step in range(4):
                        if SPLIT_AT[kind(first, u)][step] == (q, s) and not last_tile:
                            split(t + 1, 1 - u, step)

            def pair(i, first, last):
                for u in range(2):
                    for q in range(CHUNKS):
                        chunk(2 * i + u, u, q, first, last and u == 1, not (first and (u, q) == (0, 0)))

            for step in range(4):
                split(0, 0, step)
            by_pairs(dve, pair)
            diagonal(CHUNKS * TILES - 1, 3, 1)
            for s in (5, 6):
                rest(CHUNKS * TILES - 1, 3, s)

        @block.scalar
        def _(act):
            act.wait_ge(bias_in, 16)
            nc.scalar.copy(y_sb[:, 0, 0:1], bt2_sb[0:1, 0:1]).then_inc(top_ready, 1)

            def keep_xt(t, u, half):
                act.wait_ge(xt_turned, 2 * t + half + 1)
                if half == 0:
                    wait(act, xg_picked, CHUNKS * (t - 1))
                nc.scalar.copy(xt_sb[:, u, :, 8 * half:8 * half + 8],
                               turn_bf[0:STACK, :].rearrange("k (d b) -> k b d", d=8)).then_inc(xt_ready, 1)

            def keep_a(c, q):
                act.wait_ge(a_picked, c + 1)
                wait(act, z_ready, STEPS * (c - 1))
                nc.scalar.copy(a_sb[:, q % 2, :], ring[2][0:STACK, :]).then_inc(a_ready, 1)

            def keep_zh(c, q, s):
                rows, slot = ROWS[s], (q * STEPS + s) % Z_RING
                act.wait_ge(z_ready, STEPS * c + s + 1)
                wait(act, w0_done, STEPS * c + s - Z_RING + 1)
                nc.scalar.copy(z_hi[0:rows, slot, :], z_sb[0:rows, slot, :]).then_inc(zh_ready, 1)

            def keep_x1t(c, q):
                act.wait_ge(w0_done, STEPS * (c + 1))
                wait(act, x1_turned, c)
                nc.scalar.copy(x1t_sb[:, :], acc[q % 2][:, :]).then_inc(x1t_ready, 1)

            def keep_x1g(c):
                act.wait_ge(x1_turned, c + 1)
                wait(act, g_done, GROUPS * c)
                nc.scalar.copy(x1g_sb[:, :, :], turn[:, :].rearrange("p (g n) -> p g n", g=GROUPS)
                               ).then_inc(x1g_ready, 1)

            def keep_g(t, u, q, g):
                act.wait_ge(g_done, GROUPS * (CHUNKS * t + q) + g + 1)
                b0 = (q * GROUPS + g) * GROUP
                nc.scalar.copy(g_sb[:, u, :, b0:b0 + GROUP].rearrange("n m b -> n b m"),
                               g_ps[:, 0:GROUP * EXT].rearrange("n (b m) -> n b m", m=EXT)).then_inc(g_ready, 1)

            def keep_z2(t):
                act.wait_ge(top_done, 4 * t + 1)
                nc.scalar.copy(z2_sb[:, :], top_ps[:, 0:TILE]).then_inc(top_ready, 1)

            def keep_h1(t):
                act.wait_ge(top_done, 4 * t + 2)
                nc.scalar.activation(h1_sb[:, :, :].rearrange("p k b -> p (k b)"), top_ps[:, :],
                                     ACT.Relu).then_inc(top_ready, 1)

            def keep_h2(t):
                act.wait_ge(top_done, 4 * t + 3)
                for k in range(H2 // 128):
                    nc.scalar.activation(h2_sb[:, k, :], top_ps[:, k * TILE:(k + 1) * TILE], ACT.Relu,
                                         bias=bt2_sb[:, k:k + 1]).then_inc(top_ready, 1)

            def keep_y(t):
                act.wait_ge(top_done, 4 * t + 4)
                nc.scalar.copy(y_sb[:, bass.ds(t, 1), :].rearrange("p t b -> p (t b)"),
                               top_ps[0:1, 0:TILE]).then_inc(top_ready, 1)

            def place(t, u, q, back):
                return (t, u, q - back) if q >= back else (t - 1, 1 - u, q - back + CHUNKS)

            def chunk(i, u, q, first, last):
                t = 2 * i + u
                c = CHUNKS * t + q
                last_tile = last and u == 1
                has_before = not (first and (u, q) == (0, 0))
                has_two_before = has_before and not (first and (u, q) == (0, 1))
                with_a = not (last_tile and q == 3)
                tile_0 = first and u == 0

                def behind(q, s):
                    if (q, s) in TURN_AT[kind(first, u)] and not last_tile:
                        keep_xt(t + 1, 1 - u, TURN_AT[kind(first, u)].index((q, s)))
                    if (q, s) == SUM_END and not tile_0:
                        keep_z2(t - 1)
                    if not first:
                        if (q, s) == H1_AT[-1]:
                            keep_h1(t - 2)
                        if (q, s) == H2_AT[-1]:
                            keep_h2(t - 2)
                        if (q, s) == Y_AT:
                            keep_y(t - 2)

                keep_zh(c, q, 0)
                if has_two_before:
                    keep_g(*place(t, u, q, 2), 3)
                if q:
                    behind(q - 1, 5)
                keep_zh(c, q, 1)
                if has_before:
                    keep_x1t(c - 1, (q - 1) % CHUNKS)
                if q:
                    behind(q - 1, 6)
                keep_zh(c, q, 2)
                if has_before:
                    keep_x1g(c - 1)
                behind(q, 0)
                keep_zh(c, q, 3)
                behind(q, 1)
                if with_a and not late_a(first, u, q):
                    keep_a(c + 1, (q + 1) % CHUNKS)
                for s in (4, 5, 6):
                    keep_zh(c, q, s)
                    if s == 6 and late_a(first, u, q):
                        keep_a(c + 1, 0)
                    if has_before:
                        keep_g(*place(t, u, q, 1), s - 4)
                    behind(q, s - 2)

            def pair(i, first, last):
                for u in range(2):
                    for q in range(CHUNKS):
                        chunk(i, u, q, first, last)

            keep_xt(0, 0, 0)
            keep_xt(0, 0, 1)
            keep_a(0, 0)
            by_pairs(act, pair)
            keep_g(TILES - 1, 1, 2, 3)
            keep_x1t(CHUNKS * TILES - 1, 3)
            keep_x1g(CHUNKS * TILES - 1)
            keep_h1(TILES - 2)
            for g in range(GROUPS):
                keep_g(TILES - 1, 1, 3, g)
            keep_h2(TILES - 2)
            keep_y(TILES - 2)
            keep_z2(TILES - 1)
            keep_h1(TILES - 1)
            keep_h2(TILES - 1)
            keep_y(TILES - 1)

        @block.tensor
        def _(pe):
            def turn_xt(t, half, c):
                if half == 0:
                    pe.wait_ge(split_step, 4 * t + 4)
                    wait(pe, x1g_ready, c)
                else:
                    pe.wait_ge(xt_ready, 2 * t + 1)
                for d in range(8):
                    last = nc.tensor.transpose(turn_bf[0:STACK, d * TILE:(d + 1) * TILE],
                                               parts_sb[:, 8 * half + d, :], ident_bf[:, :])
                last.then_inc(xt_turned, 1)

            def chunk_of_x(u, q):
                return xt_sb[:, u, PART * q:PART * (q + 1), :].rearrange("k b d -> k (b d)")

            def pick_a(u, q):
                nc.tensor.matmul(ring[2][0:STACK, :], copies_sb, chunk_of_x(u, q),
                                 start=True, stop=True).then_inc(a_picked, 1)

            def pick_b(u, q, s):
                k0 = sum(ROWS[:s])
                nc.tensor.matmul(ring[(0, 1, 2, 0, 1, 0, 1)[s]][0:ROWS[s], :], pick_sb[:, k0:k0 + ROWS[s]],
                                 chunk_of_x(u, q), start=True, stop=True).then_inc(b_picked, 1)

            def weigh(c, q, s):
                pe.wait_ge(zl_ready, STEPS * c + s + 1)
                if s == 0:
                    wait(pe, x1t_ready, c - 1)
                rows, slot = ROWS[s], (q * STEPS + s) % Z_RING
                terms = [(w0_lo, z_hi), (w0_hi, z_hi), (w0_hi, z_lo)]
                for n, (w, z) in enumerate(terms):
                    last = nc.tensor.matmul(acc[q % 2][:, :], w[0:rows, s, :], z[0:rows, slot, :],
                                            start=(s == 0 and n == 0), stop=(s == STEPS - 1 and n == 2))
                last.then_inc(w0_done, 1)

            def pick_x(u, q):
                for g in range(GROUPS):
                    b0 = (q * GROUPS + g) * GROUP
                    last = nc.tensor.matmul(ring[2][:, g * FIELDS:(g + 1) * FIELDS],
                                            xt_sb[:, u, b0:b0 + GROUP, :].rearrange("k b d -> k (b d)"),
                                            pick_sb[:, (len(OFFSETS) - 1) * FIELDS:], start=True, stop=True)
                last.then_inc(xg_picked, 1)

            def turn_x1(c, xt_halves):
                pe.wait_ge(x1t_ready, c + 1)
                if xt_halves is not None:
                    pe.wait_ge(xt_ready, xt_halves)
                else:
                    wait(pe, x1g_ready, c)
                for g in range(GROUPS):
                    last = nc.tensor.transpose(turn[:, g * OUT:(g + 1) * OUT],
                                               x1t_sb[:, g * 128:(g + 1) * 128], ident_sb[:, :])
                last.then_inc(x1_turned, 1)

            def g_group(c, q, g):
                if g == 0:
                    pe.wait_ge(x1g_ready, c + 1)
                if g % 2 == 0:
                    pe.wait_ge(xd_ready, 2 * c + g // 2 + 1)
                wait(pe, g_ready, GROUPS * c + g)
                nc.tensor.matmul(g_ps[:, 0:GROUP * EXT], x1g_sb[:, g, :],
                                 xd_sb[:, q % 2, g, :, :].rearrange("p b m -> p (b m)"),
                                 start=True, stop=True).then_inc(g_done, 1)

            def sum_x2(t, u, m0, m1):
                if m0 == 0:
                    pe.wait_ge(top_ready, 5 * t + 1)
                    pe.wait_ge(g_ready, CHUNKS * GROUPS * (t + 1))
                for m in range(m0, m1):
                    last = nc.tensor.matmul(top_ps[:, 0:TILE], w1_sb[:, m, :], g_sb[:, u, m, :],
                                            start=(m == 0), stop=(m == FIELDS - 1))
                if m1 == FIELDS:
                    last.then_inc(top_done, 1)

            def hidden_1(t, u, k):
                if k == 0:
                    pe.wait_ge(top_ready, 5 * t + 2)
                h = slice(k * 128, (k + 1) * 128)
                dst = top_ps[:, k * TILE:(k + 1) * TILE]
                nc.tensor.matmul(dst, wt1_sb[:, 0, h], g_sb[:, u, FIELDS, :], start=True, stop=False)
                nc.tensor.matmul(dst, wt1_sb[:, 1, h], z2_sb[:, :], start=False, stop=False)
                last = nc.tensor.matmul(dst, wt1_ctx[:, h], ctx_sb[:, bass.ds(t * TILE, TILE)],
                                        start=False, stop=True)
                if k == H1 // 128 - 1:
                    last.then_inc(top_done, 1)

            def hidden_2(t, k):
                if k == 0:
                    pe.wait_ge(top_ready, 5 * t + 3)
                for n in range(H1 // 128):
                    last = nc.tensor.matmul(top_ps[:, k * TILE:(k + 1) * TILE], wt2_sb[:, n, k * 128:(k + 1) * 128],
                                            h1_sb[:, n, :], start=(n == 0), stop=(n == H1 // 128 - 1))
                if k == H2 // 128 - 1:
                    last.then_inc(top_done, 1)

            def output(t):
                pe.wait_ge(top_ready, 5 * t + 5)
                for n in range(H2 // 128):
                    last = nc.tensor.matmul(top_ps[0:1, 0:TILE], wt3_sb[:, n:n + 1], h2_sb[:, n, :],
                                            start=(n == 0), stop=(n == H2 // 128 - 1))
                last.then_inc(top_done, 1)

            def last_layers(t, u, q, s, first):
                if (q, s) in SUM_AT and not (first and u == 0):
                    m0 = sum(n for at, n in SUM_AT.items() if at < (q, s))
                    sum_x2(t - 1, 1 - u, m0, m0 + SUM_AT[q, s])
                if (q, s) == H1_AT[0] and not (first and u == 0):
                    hidden_1(t - 1, 1 - u, 0)
                if first:
                    return
                if (q, s) in H1_AT[1:]:
                    hidden_1(t - 2, u, H1_AT.index((q, s)))
                if (q, s) in H2_AT:
                    hidden_2(t - 2, H2_AT.index((q, s)))
                if (q, s) == Y_AT:
                    output(t - 2)

            def chunk(i, u, q, first, last):
                t = 2 * i + u
                c = CHUNKS * t + q
                last_tile = last and u == 1
                nxt_u, nxt_q = (u, q + 1) if q < 3 else (1 - u, 0)
                more = not (last_tile and q == 3)
                has_before = not (first and (u, q) == (0, 0))
                a_late = late_a(first, u, q)

                def side(s):
                    if has_before and s == 0:
                        if q == 3 and not (last_tile or late_a(first, u, q)):
                            turn_x1(c - 1, 2 * t + 4)
                        else:
                            turn_x1(c - 1, 2 * t + 2 if first and (u, q) == (1, 0) else None)
                    if has_before and s >= 2 and s < 6:
                        g_group(c - 1, (q - 1) % 4, s - 2)
                    if (q, s) in TURN_AT[kind(first, u)] and not last_tile:
                        turn_xt(t + 1, TURN_AT[kind(first, u)].index((q, s)), c)
                    last_layers(t, u, q, s, first)

                def next_a():
                    if q == 3:
                        pe.wait_ge(xt_ready, 2 * t + 4)
                    pick_a(nxt_u, nxt_q)

                for s in range(STEPS):
                    if s == 0:
                        pe.wait_ge(z_ready, STEPS * c + 1)
                        pick_b(u, q, 3)
                    elif s == 1:
                        pe.wait_ge(z_ready, STEPS * c + 2)
                        pick_b(u, q, 4)
                    elif s == 2:
                        pe.wait_ge(z_ready, STEPS * c + 3)
                        if a_late or not more:
                            pick_x(u, q)
                        else:
                            next_a()
                        pe.wait_ge(z_ready, STEPS * c + 4)
                        pick_b(u, q, 5)
                    elif s == 3:
                        pe.wait_ge(z_ready, STEPS * c + 5)
                        pick_b(u, q, 6)
                    elif s == 4 and more:
                        if a_late:
                            pe.wait_ge(xd_ready, 2 * (c + 1))
                            next_a()
                        else:
                            pe.wait_ge(a_ready, c + 2)
                            pick_x(u, q)
                        pe.wait_ge(z_ready, STEPS * c + 6)
                        pick_b(nxt_u, nxt_q, 0)
                    elif s == 5 and more:
                        pe.wait_ge(z_ready, STEPS * c + 7)
                        pick_b(nxt_u, nxt_q, 1)
                    elif s == 6 and more:
                        if a_late:
                            pe.wait_ge(a_ready, c + 2)
                        else:
                            pe.wait_ge(xd_ready, 2 * (c + 1))
                        pick_b(nxt_u, nxt_q, 2)
                    if s:
                        side(s - 1)
                    weigh(c, q, s)
                side(STEPS - 1)

            def begin(t, u):
                pe.wait_ge(xt_ready, 2 * t + 2)
                wait(pe, xd_ready, 2 * CHUNKS * t)
                pick_a(u, 0)
                wait(pe, z_ready, STEPS * CHUNKS * t)
                pick_b(u, 0, 0)
                pick_b(u, 0, 1)
                pe.wait_ge(a_ready, CHUNKS * t + 1)
                pick_b(u, 0, 2)

            def pair(i, first, last):
                for u in range(2):
                    for q in range(CHUNKS):
                        chunk(i, u, q, first, last)

            pe.wait_ge(ident_bf_ready, 1)
            turn_xt(0, 0, 0)
            turn_xt(0, 1, 0)
            pe.wait_ge(pick_ready, 1)
            pe.wait_ge(w0_folded, 6)
            pe.wait_ge(mask_set, 2 * GROUPS)
            pe.wait_ge(top_in, 96)
            begin(0, 0)
            by_pairs(pe, pair)
            for k in range(1, 4):
                hidden_1(TILES - 2, 0, k)
            turn_x1(CHUNKS * TILES - 1, None)
            for k in range(2):
                hidden_2(TILES - 2, k)
            for g in range(GROUPS):
                g_group(CHUNKS * TILES - 1, 3, g)
            output(TILES - 2)
            sum_x2(TILES - 1, 1, 0, FIELDS)
            for k in range(4):
                hidden_1(TILES - 1, 1, k)
            for k in range(2):
                hidden_2(TILES - 1, k)
            output(TILES - 1)


def _constants():
    pick = np.zeros((3, FIELDS, len(OFFSETS), FIELDS), np.float32)
    for n, k in enumerate(OFFSETS):
        for m in range(FIELDS):
            pick[:, (m + k) % FIELDS, n, m] = 1
    copies = np.zeros((3, FIELDS, 3, FIELDS), np.float32)
    for m in range(FIELDS):
        copies[:, m, :, m] = 1
    mask = np.zeros((GROUP, DIM, GROUP), np.float32)
    for b in range(GROUP):
        mask[b, :, b] = 1
    return {"pick": np.concatenate([pick.reshape(STACK, -1), copies.reshape(STACK, -1)], 1),
            "ident": np.eye(128, dtype=np.float32), "mask": mask.reshape(128, GROUP)}


def kernel(**inputs):
    import concourse.bacc as _bacc
    from concourse.bass_utils import run_bass_kernel_spmd as _run

    nc = _bacc.Bacc("TRN2", target_bir_lowering=False, num_devices=1)
    w0 = np.asarray(inputs["L0_rec_W0"]).reshape(FIELDS, FIELDS, OUT)
    m = np.arange(FIELDS)
    wt1 = np.asarray(inputs["W_top1"])
    arrays = {
        "in_ctx_t": np.concatenate([np.asarray(inputs["dense_ctx"]).T, np.ones((1, BATCH), np.float32)]),
        "in_ids": np.asarray(inputs["ids"]),
        "in_w0_mn": np.concatenate([w0[m, (m + k) % FIELDS] for k in OFFSETS]),
        "in_w0_nm": np.concatenate([w0[(m + k) % FIELDS, m] for k in OFFSETS if k]),
        "in_w1": np.asarray(inputs["L0_rec_W1"]),
        "in_wt1": wt1[:2 * OUT], "in_wt1_rest": np.concatenate([wt1[2 * OUT:], np.asarray(inputs["b_top1"])[None]]),
        "in_wt2": np.asarray(inputs["W_top2"]), "in_bt2": np.asarray(inputs["b_top2"]).reshape(-1, 128).T,
        "in_wt3": np.asarray(inputs["W_top3"]).reshape(-1, 128).T,
    }
    arrays.update({f"in_{n}": a for n, a in _constants().items()})
    arrays.update({f"in_tbl_{f}": np.asarray(inputs[f"tbl_{f}"]) for f in range(FIELDS)})
    arrays = {n: np.ascontiguousarray(a) for n, a in arrays.items()}
    ap = {n[3:]: nc.dram_tensor(n, a.shape, mybir.dt.from_np(a.dtype), kind="ExternalInput").ap()
          for n, a in arrays.items()}
    out = nc.dram_tensor("out_y", (1, BATCH), mybir.dt.float32, kind="ExternalOutput").ap()
    build(nc, ap["ctx_t"], ap["ids"], [ap[f"tbl_{f}"] for f in range(FIELDS)], ap["w0_mn"], ap["w0_nm"],
          ap["w1"], ap["wt1"], ap["wt1_rest"], ap["wt2"], ap["bt2"], ap["wt3"],
          ap["pick"], ap["ident"], ap["mask"], out)
    r = _run(nc, [arrays], core_ids=[0])
    return np.asarray(r.results[0]["out_y"]).reshape(BATCH, 1)
```

```python
from contextlib import ExitStack

import numpy as np
import concourse.bass as bass
import concourse.mybir as mybir

FIELDS, DIM, BATCH, OUT = 39, 16, 1024, 128
TILE = 128
TILES, PAIRS = BATCH // TILE, BATCH // TILE // 2
CHUNKS = 4
COLS = TILE * DIM // CHUNKS
TURNS = (13, 0, 26)
SHIFTS = list(range(7))
STEPS = len(SHIFTS)
STACK = len(TURNS) * FIELDS
ROWS = [STACK if shift else 2 * FIELDS for shift in SHIFTS]
HEIGHT = STACK + max(SHIFTS) + 1
DS = 4
GROUP = 128 // DIM
GROUPS = 4
PART = 32
EXT = FIELDS + 1
CTX, H1, H2 = 16, 512, 256
HALF, CTX_PARTS = BATCH // 2, 2 * H1 // 128
CTX_EARLY = 6
Z_RING = 4
SUM_AT = {(1, 3): 3, (1, 4): 3, (1, 5): 3, (1, 6): 4,
          (2, 0): 3, (2, 1): 2, (2, 2): 1, (2, 3): 2, (2, 4): 1, (2, 5): 1, (2, 6): 1,
          (3, 0): 3, (3, 1): 3, (3, 2): 3, (3, 3): 3, (3, 4): 3}
SUM_END = max(SUM_AT)
H1_AT = [(3, 6), (0, 0), (0, 1), (0, 2)]
ADD_AT = (0, 6)
KEEP_H1_AT = (0, 4)
H2_AT = [(0, 5), (0, 6)]
Y_AT = (1, 1)
REPEAT_AT = {True: (2, 6), False: (2, 5)}
TURN_AT = {True: [(2, 3), (2, 5)], False: [(2, 5), (2, 6)]}
B_GROUPS = [1, 3]
BLOCK = 10
PER_BANK = 3


def is_small(rows):
    return rows % BLOCK == 0 and rows <= 128 * BLOCK


def build(nc, ctx_t, ids, small_ids, tables, w0_mn, w0_nm, w1, wt1, wt1_rest, wt2, bt2, wt3,
          ident, consts, out):
    f32, f32r, i32 = mybir.dt.float32, mybir.dt.float32r, mybir.dt.int32
    ALU, ACT = mybir.AluOpType, mybir.ActivationFunctionType

    small = sum(is_small(table.shape[0]) for table in tables)
    banks = small // PER_BANK
    assert small == banks * PER_BANK

    with ExitStack() as ctx:
        def sbuf(name, shape, dt=f32):
            return ctx.enter_context(nc.sbuf_tensor(name, shape, dt))

        def sem(name):
            return ctx.enter_context(nc.semaphore(name))

        w0_sb = sbuf("w0_sb", [STACK, STEPS, OUT])
        w0_other = sbuf("w0_other", [STACK, STEPS, OUT])
        w0_hi = sbuf("w0_hi", [STACK, STEPS, OUT], f32r)
        w0_lo = sbuf("w0_lo", [STACK, STEPS, OUT], f32r)
        w1_sb = sbuf("w1_sb", [OUT, FIELDS, OUT])
        wt1_sb = sbuf("wt1_sb", [128, 2, H1])
        wt2_sb = sbuf("wt2_sb", [128, H1 // 128, H2])
        wt3_sb = sbuf("wt3_sb", [128, H2 // 128])
        bt2_sb = sbuf("bt2_sb", [128, H2 // 128])
        ident_sb = sbuf("ident_sb", [128, 128])
        consts_sb = sbuf("consts_sb", [128, GROUP + BLOCK + 1])
        mask_sb = consts_sb[:, 0:GROUP]
        numbers_sb = consts_sb[:, GROUP:GROUP + BLOCK]
        middle_sb = consts_sb[:, GROUP + BLOCK:]
        ids_sb = sbuf("ids_sb", [TILE, TILES, FIELDS], i32)
        ids_now = sbuf("ids_now", [TILE, 2, FIELDS], i32)
        rows_sb = sbuf("rows_sb", [TILE, 2, HEIGHT * DIM])
        gate_sb = sbuf("gate_sb", [1, 2])
        s_sb = sbuf("s_sb", [HEIGHT, 2, TILE, DIM])
        a_sb = sbuf("a_sb", [STACK, 2, COLS])
        z_sb = sbuf("z_sb", [STACK, Z_RING, COLS])
        z_hi = sbuf("z_hi", [STACK, Z_RING, COLS], f32r)
        z_lo = sbuf("z_lo", [STACK, Z_RING, COLS], f32r)
        x1t_sb = sbuf("x1t_sb", [OUT, COLS])
        x1g_sb = sbuf("x1g_sb", [128, GROUPS, OUT])
        xd_sb = sbuf("xd_sb", [128, 2, GROUPS, GROUP, EXT])
        z2_sb = sbuf("z2_sb", [OUT, TILE])
        ctx_h1 = sbuf("ctx_h1", [128, H1 // 128, BATCH])
        h1_sum = sbuf("h1_sum", [128, H1 // 128, TILE])
        h1_sb = sbuf("h1_sb", [128, H1 // 128, TILE])
        h2_sb = sbuf("h2_sb", [128, H2 // 128, TILE])
        y_sb = sbuf("y_sb", [1, TILES, TILE])

        with ExitStack() as early:
            def small_sbuf(name, shape, dt=f32):
                return early.enter_context(nc.sbuf_tensor(name, shape, dt))

            small_sb = small_sbuf("small_sb", [128, small, BLOCK * DIM + 1])
            small_ids_sb = small_sbuf("small_ids_sb", [128, small * TILE], i32)
            far_sb = small_sbuf("far_sb", [128, small * TILE])
            hot_sb = small_sbuf("hot_sb", [128, small * TILE])
            small_ids_f = small_sbuf("small_ids_f", [TILE, small])
            row_sb = small_sbuf("row_sb", [TILE, PER_BANK])
            row_hot_sb = small_sbuf("row_hot_sb", [TILE, PER_BANK, BLOCK])
            wt1_ctx = small_sbuf("wt1_ctx", [CTX + 1, H1])
            ctx_sb = small_sbuf("ctx_sb", [CTX + 1, BATCH])
            block_sb = small_sbuf("block_sb", [TILE, PER_BANK, BLOCK, DIM])
        b_sb = sbuf("b_sb", [STACK, 2, STEPS - 1, COLS])
        g_sb = sbuf("g_sb", [OUT, 2, EXT, TILE])

        acc = [ctx.enter_context(nc.psum_tensor(f"acc{k}", [128, COLS], f32)) for k in range(2)]
        turn = ctx.enter_context(nc.psum_tensor("turn", [128, COLS], f32))
        s_ps = [ctx.enter_context(nc.psum_tensor(f"s_ps{k}", [128, COLS], f32)) for k in range(2)]
        xg_ps = ctx.enter_context(nc.psum_tensor("xg_ps", [128, COLS], f32))
        g_ps = ctx.enter_context(nc.psum_tensor("g_ps", [128, COLS], f32))
        top_ps = ctx.enter_context(nc.psum_tensor("top_ps", [128, COLS], f32))
        hot_bank = [*acc, turn, *s_ps, xg_ps]
        first_s_ps = [*s_ps, g_ps, top_ps]

        ids_in = sem("ids_in")
        w0_in = sem("w0_in")
        consts_in = sem("consts_in")
        ident_in = sem("ident_in")
        small_ids_in = sem("small_ids_in")
        small_in = sem("small_in")
        far_ready = sem("far_ready")
        hot_ready = sem("hot_ready")
        middle_set = sem("middle_set")
        ids_cast = sem("ids_cast")
        row_step = sem("row_step")
        blocks_picked = sem("blocks_picked")
        block_masked = sem("block_masked")
        small_rows = sem("small_rows")
        top_in = sem("top_in")
        bias_in = sem("bias_in")
        ctx_in = sem("ctx_in")
        ctx_done = sem("ctx_done")
        ctx_ready = sem("ctx_ready")
        h1_added = sem("h1_added")
        w0_folded = sem("w0_folded")
        mask_set = sem("mask_set")
        ids_copied = sem("ids_copied")
        gate_passed = sem("gate_passed")
        gathered = [sem("gathered_even"), sem("gathered_odd")]
        rows_repeated = sem("rows_repeated")
        s_turned = sem("s_turned")
        s_ready = sem("s_ready")
        a_in = [sem("a_in_even"), sem("a_in_odd")]
        b_in = [[sem("b_early_in_even"), sem("b_later_in_even")], [sem("b_early_in_odd"), sem("b_later_in_odd")]]
        z_ready = sem("z_ready")
        zh_ready = sem("zh_ready")
        zl_ready = sem("zl_ready")
        w0_done = sem("w0_done")
        x1t_ready = sem("x1t_ready")
        x1_turned = sem("x1_turned")
        x1g_ready = sem("x1g_ready")
        xg_turned = sem("xg_turned")
        xd_ready = sem("xd_ready")
        g_done = sem("g_done")
        g_ready = sem("g_ready")
        top_done = sem("top_done")
        top_ready = sem("top_ready")
        stored = sem("stored")

        def wait(engine, semaphore, value):
            if isinstance(value, int) and value <= 0:
                return
            engine.wait_ge(semaphore, value)

        def all_gathered(i, u):
            return 16 * (FIELDS * (i + 1) - (small if u == 0 else 0))

        def by_pairs(engine, pair):
            pair(0, True, False)
            with engine.Fori(1, PAIRS - 1) as i:
                pair(i, False, False)
            pair(PAIRS - 1, False, True)

        block = ctx.enter_context(nc.Block())

        @block.sync
        def _(sp):
            sp.dma_start(ids_sb[:, :, :], ids.rearrange("(t p) f -> p t f", p=TILE)).then_inc(ids_in, 16)
            sp.dma_start(small_ids_sb[:, :], small_ids.to_broadcast([128, small * TILE])
                         ).then_inc(small_ids_in, 16)
            sp.dma_start(consts_sb[:, :], consts).then_inc(consts_in, 16)
            for f in range(small):
                blocks = tables[f].shape[0] // BLOCK
                sp.dma_start(small_sb[0:blocks, f, 0:BLOCK * DIM], tables[f].rearrange("(p h) d -> p (h d)", h=BLOCK)
                             ).then_inc(small_in, 16)
            sp.dma_start(wt1_ctx[:, :], wt1_rest).then_inc(ctx_in, 16)
            sp.dma_start(ctx_sb[:, :], ctx_t).then_inc(ctx_in, 16)
            sp.dma_start(ident_sb[:, :], ident).then_inc(ident_in, 16)
            for weights, dst in ((w0_mn, w0_sb), (w0_nm, w0_other)):
                short = weights.shape[0] - (STEPS - 1) * STACK
                sp.dma_start(dst[0:short, 0, :], weights[0:short, :]).then_inc(w0_in, 16)
                sp.dma_start(dst[:, 1:, :],
                             weights[short:, :].rearrange("(t p) o -> p t o", p=STACK)).then_inc(w0_in, 16)
            sp.dma_start(w1_sb[:, :, :], w1.rearrange("(m n) o -> n m o", n=OUT)).then_inc(top_in, 16)
            sp.dma_start(wt1_sb[:, :, :], wt1.rearrange("(c p) h -> p c h", p=128)).then_inc(top_in, 16)
            sp.dma_start(wt2_sb[:, :, :], wt2.rearrange("(c p) h -> p c h", p=128)).then_inc(top_in, 16)
            sp.dma_start(wt3_sb[:, :], wt3).then_inc(top_in, 16)
            sp.dma_start(bt2_sb[:, :], bt2).then_inc(bias_in, 16)

            def chunk(t, u, q):
                c = CHUNKS * t + q
                if q == 0:
                    sp.wait_ge(s_ready, 4 * (t + 1))
                wait(sp, z_ready, STEPS * (c - 1))
                columns = slice(PART * q, PART * (q + 1))
                for j, turned in enumerate(TURNS):
                    sp.dma_start(a_sb[j * FIELDS:(j + 1) * FIELDS, q % 2, :],
                                 s_sb[turned:turned + FIELDS, u, columns, :].rearrange("r b d -> r (b d)")
                                 ).then_inc(a_in[q % 2], 16)
                for k in range(1, STEPS):
                    sp.dma_start(b_sb[:, q % 2, k - 1, :],
                                 s_sb[SHIFTS[k]:SHIFTS[k] + STACK, u, columns, :].rearrange("r b d -> r (b d)")
                                 ).then_inc(b_in[q % 2][k >= B_GROUPS[1]], 16)

            def pair(i, first, last):
                for u in range(2):
                    for q in range(CHUNKS):
                        chunk(2 * i + u, u, q)

            by_pairs(sp, pair)
            sp.wait_ge(top_ready, 5 * TILES + 1)
            sp.dma_start(out, y_sb[:, :, :].rearrange("p j b -> p (j b)")).then_inc(stored, 16)
            sp.wait_ge(stored, 16)

        @block.gpsimd
        def _(pool):
            nc.gpsimd.memset(gate_sb[:, :], 0.0).then_inc(gate_passed, 1)
            pool.wait_ge(ids_in, 16)

            def pair(i, first, last):
                for u in range(2):
                    t = 2 * i + u
                    wait(pool, gathered[u], all_gathered(i - 1, u) if not first else 0)
                    nc.gpsimd.tensor_copy(ids_now[:, u, :], ids_sb[:, bass.ds(t, 1), :].rearrange(
                        "p t f -> p (t f)")).then_inc(ids_copied, 1)
                    pool.wait_ge(gate_passed, t + 1)
                    wait(pool, s_turned, 4 * (t - 1))
                    pool.wait_ge(ids_copied, t + 1)
                    nc.gpsimd.tensor_tensor(gate_sb[:, 1:2], gate_sb[:, 0:1], gate_sb[:, 0:1],
                                            ALU.add).then_inc(gate_passed, 1)
                    for f in range(small if first and u == 0 else 0, FIELDS):
                        nc.gpsimd.indirect_dma_start(
                            rows_sb[:, u, f * DIM:(f + 1) * DIM], None, tables[f],
                            bass.IndirectOffsetOnAxis(ap=ids_now[:, u, f:f + 1], axis=0)).then_inc(gathered[u], 16)

            by_pairs(pool, pair)

        @block.vector
        def _(dve):
            def small_setup():
                dve.wait_ge(consts_in, 16)
                nc.vector.tensor_copy(small_sb[:, :, BLOCK * DIM], middle_sb.to_broadcast([128, small])
                                      ).then_inc(middle_set, 1)
                dve.wait_ge(ids_in, 16)
                nc.vector.tensor_copy(small_ids_f[:, :], ids_sb[:, 0, 0:small]).then_inc(ids_cast, 1)

            def small_hot():
                dve.wait_ge(far_ready, 1)
                nc.vector.tensor_scalar(hot_sb[:, :], far_sb[:, :], BLOCK / 2, None, ALU.is_lt).then_inc(hot_ready, 1)

            def small_select():
                for n in range(banks):
                    fields = slice(n * PER_BANK, (n + 1) * PER_BANK)
                    blocks = hot_bank[n][:, 0:PER_BANK * (BLOCK * DIM + 1)].rearrange("p (f x) -> p f x", f=PER_BANK)
                    dve.wait_ge(blocks_picked, n + 1)
                    dve.wait_ge(ids_cast, 1)
                    wait(dve, row_step, 2 * n)
                    nc.vector.tensor_tensor(row_sb[:, :], small_ids_f[:, fields], blocks[:, :, BLOCK * DIM],
                                            ALU.add).then_inc(row_step, 1)
                    dve.wait_ge(row_step, 2 * n + 1)
                    wait(dve, block_masked, n)
                    shape = [TILE, PER_BANK, BLOCK]
                    nc.vector.tensor_tensor(row_hot_sb[:, :, :], row_sb[:, :].unsqueeze(2).to_broadcast(shape),
                                            numbers_sb.unsqueeze(1).to_broadcast(shape), ALU.is_equal
                                            ).then_inc(row_step, 1)
                    dve.wait_ge(row_step, 2 * n + 2)
                    wait(dve, small_rows, n)
                    nc.vector.tensor_tensor(
                        block_sb[:, :, :, :], blocks[:, :, 0:BLOCK * DIM].rearrange("p f (h d) -> p f h d", h=BLOCK),
                        row_hot_sb[:, :, :].unsqueeze(3).to_broadcast([TILE, PER_BANK, BLOCK, DIM]),
                        ALU.mult).then_inc(block_masked, 1)
                    dve.wait_ge(block_masked, n + 1)
                    nc.vector.tensor_reduce(
                        rows_sb[:, 0, fields.start * DIM:fields.stop * DIM].rearrange("p (f d) -> p f d", d=DIM),
                        block_sb[:, :, :, :].rearrange("p f h d -> p f d h"),
                        mybir.AxisListType.X, ALU.add).then_inc(small_rows, 1)

            def fold_weights():
                dve.wait_ge(w0_in, 64)
                nc.vector.tensor_tensor(w0_sb[:, 1:, :], w0_sb[:, 1:, :], w0_other[:, 1:, :],
                                        ALU.add).then_inc(w0_folded, 1)
                nc.vector.tensor_tensor(w0_sb[0:FIELDS, 0, :], w0_sb[0:FIELDS, 0, :],
                                        w0_other[0:FIELDS, 0, :], ALU.add).then_inc(w0_folded, 1)
                dve.wait_ge(w0_folded, 2)
                rows = ROWS[0]
                nc.vector.tensor_copy(w0_hi[:, 1:, :], w0_sb[:, 1:, :]).then_inc(w0_folded, 1)
                nc.vector.tensor_copy(w0_hi[0:rows, 0, :], w0_sb[0:rows, 0, :]).then_inc(w0_folded, 1)
                dve.wait_ge(w0_folded, 4)
                nc.vector.tensor_tensor(w0_lo[:, 1:, :], w0_sb[:, 1:, :], w0_hi[:, 1:, :].bitcast(f32),
                                        ALU.subtract).then_inc(w0_folded, 1)
                nc.vector.tensor_tensor(w0_lo[0:rows, 0, :], w0_sb[0:rows, 0, :],
                                        w0_hi[0:rows, 0, :].bitcast(f32), ALU.subtract).then_inc(w0_folded, 1)

            def repeat(u):
                size = FIELDS * DIM
                copies = rows_sb[:, u, size:3 * size].rearrange("p (c x) -> p c x", c=2)
                nc.vector.tensor_copy(copies, rows_sb[:, u, 0:size].unsqueeze(1).to_broadcast([TILE, 2, size])
                                      ).then_inc(rows_repeated, 1)
                nc.vector.tensor_copy(rows_sb[:, u, 3 * size:], rows_sb[:, u, 0:HEIGHT * DIM - 3 * size]
                                      ).then_inc(rows_repeated, 1)

            def product(t, u, q, s):
                c = CHUNKS * t + q
                rows, slot = ROWS[s], (q * STEPS + s) % Z_RING
                chunks = 2 * t + q // 2 + 1
                if s == 0:
                    dve.wait_ge(a_in[q % 2], 16 * len(TURNS) * chunks)
                elif s == B_GROUPS[0]:
                    dve.wait_ge(b_in[q % 2][0], 16 * (B_GROUPS[1] - B_GROUPS[0]) * chunks)
                elif s == B_GROUPS[1]:
                    dve.wait_ge(b_in[q % 2][1], 16 * (STEPS - B_GROUPS[1]) * chunks)
                wait(dve, zl_ready, STEPS * c + s - Z_RING + 1)
                if SHIFTS[s]:
                    shifted = b_sb[:, q % 2, s - 1, :]
                else:
                    shifted = s_sb[0:rows, u, PART * q:PART * (q + 1), :].rearrange("r b d -> r (b d)")
                nc.vector.tensor_tensor(z_sb[0:rows, slot, :], shifted, a_sb[0:rows, q % 2, :],
                                        ALU.mult).then_inc(z_ready, 1)

            def rest(c, q, s):
                rows, slot = ROWS[s], (q * STEPS + s) % Z_RING
                dve.wait_ge(zh_ready, STEPS * c + s + 1)
                wait(dve, w0_done, STEPS * c + s - Z_RING + 1)
                nc.vector.tensor_tensor(z_lo[0:rows, slot, :], z_sb[0:rows, slot, :],
                                        z_hi[0:rows, slot, :].bitcast(f32), ALU.subtract).then_inc(zl_ready, 1)

            def diagonal(c, q, half):
                if half == 0:
                    dve.wait_ge(xg_turned, c + 1)
                    wait(dve, g_done, GROUPS * (c - 1))
                g0, shape = 2 * half, [128, 2, GROUP, FIELDS]
                x = xg_ps[:, g0 * FIELDS:(g0 + 2) * FIELDS].rearrange("p (g m) -> p g m", g=2)
                nc.vector.tensor_tensor(
                    xd_sb[:, q % 2, g0:g0 + 2, :, 0:FIELDS], x.unsqueeze(2).to_broadcast(shape),
                    mask_sb.unsqueeze(1).unsqueeze(3).to_broadcast(shape), ALU.mult).then_inc(xd_ready, 1)

            def add_context(t):
                dve.wait_ge(top_done, 4 * t + 2)
                dve.wait_ge(ctx_ready, CTX_PARTS)
                nc.vector.tensor_tensor(h1_sum[:, :, :], top_ps[:, :].rearrange("p (k b) -> p k b", b=TILE),
                                        ctx_h1[:, :, bass.ds(t * TILE, TILE)], ALU.add).then_inc(h1_added, 1)

            def chunk(i, u, q, first, last_tile, carried):
                t = 2 * i + u
                c = CHUNKS * t + q
                tile_0 = first and u == 0
                for s in range(STEPS):
                    product(t, u, q, s)
                    if s >= 2:
                        rest(c, q, s - 2)
                    elif carried:
                        rest(c - 1, (q - 1) % CHUNKS, s + 5)
                    if s == 6:
                        diagonal(c, q, 0)
                    if s == 0 and carried:
                        diagonal(c - 1, (q - 1) % CHUNKS, 1)
                    if (q, s) == ADD_AT and not first:
                        add_context(t - 2)
                    if (q, s) == REPEAT_AT[tile_0] and not last_tile:
                        dve.wait_ge(gathered[1 - u], all_gathered(i + u, 1 - u))
                        repeat(1 - u)

            def pair(i, first, last):
                for u in range(2):
                    for q in range(CHUNKS):
                        chunk(i, u, q, first, last and u == 1, not (first and (u, q) == (0, 0)))

            small_setup()
            small_hot()
            small_select()
            fold_weights()
            dve.wait_ge(small_rows, banks)
            dve.wait_ge(gathered[0], all_gathered(0, 0))
            repeat(0)
            for n in (1, 3):
                dve.wait_ge(s_turned, n + 1)
                nc.vector.tensor_copy(s_sb[:, 0, :, DS * n:DS * (n + 1)], first_s_ps[n][0:HEIGHT, :].rearrange(
                    "r (d b) -> r b d", d=DS)).then_inc(s_ready, 1)
            by_pairs(dve, pair)
            diagonal(CHUNKS * TILES - 1, 3, 1)
            for s in (5, 6):
                rest(CHUNKS * TILES - 1, 3, s)
            add_context(TILES - 2)
            add_context(TILES - 1)

        @block.scalar
        def _(act):
            act.wait_ge(consts_in, 16)
            act.wait_ge(small_ids_in, 16)
            nc.scalar.activation(far_sb[:, :], small_ids_sb[:, :], ACT.Abs, bias=middle_sb).then_inc(far_ready, 1)
            for half in range(2):
                for g in range(GROUPS):
                    nc.scalar.copy(xd_sb[:, half, g, :, FIELDS], mask_sb).then_inc(mask_set, 1)

            def keep_context(n0, n1):
                for n in range(n0, n1):
                    act.wait_ge(ctx_done, n + 1)
                    nc.scalar.copy(ctx_h1[:, n // 2, n % 2 * HALF:(n % 2 + 1) * HALF], (g_ps, top_ps)[n % 2][:, 0:HALF]
                                   ).then_inc(ctx_ready, 1)

            keep_context(0, CTX_EARLY)
            act.wait_ge(bias_in, 16)
            nc.scalar.copy(y_sb[:, 0, 0:1], bt2_sb[0:1, 0:1]).then_inc(top_ready, 1)

            def keep_s(t, u, n, bank):
                act.wait_ge(s_turned, 4 * t + n + 1)
                if n == 0:
                    wait(act, z_ready, STEPS * CHUNKS * (t - 1))
                    wait(act, xg_turned, CHUNKS * (t - 1))
                nc.scalar.copy(s_sb[:, u, :, DS * n:DS * (n + 1)],
                               bank[0:HEIGHT, :].rearrange("r (d b) -> r b d", d=DS)).then_inc(s_ready, 1)

            def keep_zh(c, q, s):
                rows, slot = ROWS[s], (q * STEPS + s) % Z_RING
                act.wait_ge(z_ready, STEPS * c + s + 1)
                wait(act, w0_done, STEPS * c + s - Z_RING + 1)
                nc.scalar.copy(z_hi[0:rows, slot, :], z_sb[0:rows, slot, :]).then_inc(zh_ready, 1)

            def keep_x1t(c, q):
                act.wait_ge(w0_done, STEPS * (c + 1))
                wait(act, x1_turned, c)
                nc.scalar.copy(x1t_sb[:, :], acc[q % 2][:, :]).then_inc(x1t_ready, 1)

            def keep_x1g(c):
                act.wait_ge(x1_turned, c + 1)
                wait(act, g_done, GROUPS * c)
                nc.scalar.copy(x1g_sb[:, :, :], turn[:, :].rearrange("p (g n) -> p g n", g=GROUPS)
                               ).then_inc(x1g_ready, 1)

            def keep_g(t, u, q, g):
                act.wait_ge(g_done, GROUPS * (CHUNKS * t + q) + g + 1)
                b0 = (q * GROUPS + g) * GROUP
                nc.scalar.copy(g_sb[:, u, :, b0:b0 + GROUP].rearrange("n m b -> n b m"),
                               g_ps[:, 0:GROUP * EXT].rearrange("n (b m) -> n b m", m=EXT)).then_inc(g_ready, 1)

            def keep_z2(t):
                act.wait_ge(top_done, 4 * t + 1)
                nc.scalar.copy(z2_sb[:, :], top_ps[:, 0:TILE]).then_inc(top_ready, 1)

            def keep_h1(t):
                act.wait_ge(h1_added, t + 1)
                nc.scalar.activation(h1_sb[:, :, :], h1_sum[:, :, :], ACT.Relu).then_inc(top_ready, 1)

            def keep_h2(t):
                act.wait_ge(top_done, 4 * t + 3)
                for k in range(H2 // 128):
                    nc.scalar.activation(h2_sb[:, k, :], top_ps[:, k * TILE:(k + 1) * TILE], ACT.Relu,
                                         bias=bt2_sb[:, k:k + 1]).then_inc(top_ready, 1)

            def keep_y(t):
                act.wait_ge(top_done, 4 * t + 4)
                nc.scalar.copy(y_sb[:, bass.ds(t, 1), :].rearrange("p t b -> p (t b)"),
                               top_ps[0:1, 0:TILE]).then_inc(top_ready, 1)

            def place(t, u, q, back):
                return (t, u, q - back) if q >= back else (t - 1, 1 - u, q - back + CHUNKS)

            def chunk(i, u, q, first, last):
                t = 2 * i + u
                c = CHUNKS * t + q
                last_tile = last and u == 1
                has_before = not (first and (u, q) == (0, 0))
                has_two_before = has_before and not (first and (u, q) == (0, 1))
                tile_0 = first and u == 0

                def behind(q, s):
                    if (q, s) in TURN_AT[tile_0] and not last_tile:
                        for k in range(2):
                            keep_s(t + 1, 1 - u, 2 * TURN_AT[tile_0].index((q, s)) + k, s_ps[k])
                    if (q, s) == SUM_END and not tile_0:
                        keep_z2(t - 1)
                    if not first:
                        if (q, s) == KEEP_H1_AT:
                            keep_h1(t - 2)
                        if (q, s) == H2_AT[-1]:
                            keep_h2(t - 2)
                        if (q, s) == Y_AT:
                            keep_y(t - 2)

                keep_zh(c, q, 0)
                if has_two_before:
                    keep_g(*place(t, u, q, 2), 3)
                if q:
                    behind(q - 1, 5)
                keep_zh(c, q, 1)
                if has_before:
                    keep_x1t(c - 1, (q - 1) % CHUNKS)
                if q:
                    behind(q - 1, 6)
                keep_zh(c, q, 2)
                if has_before:
                    keep_x1g(c - 1)
                behind(q, 0)
                keep_zh(c, q, 3)
                behind(q, 1)
                for s in (4, 5, 6):
                    keep_zh(c, q, s)
                    if has_before:
                        keep_g(*place(t, u, q, 1), s - 4)
                    behind(q, s - 2)

            def pair(i, first, last):
                for u in range(2):
                    for q in range(CHUNKS):
                        chunk(i, u, q, first, last)

            for n in (0, 2):
                keep_s(0, 0, n, first_s_ps[n])
            keep_context(CTX_EARLY, CTX_PARTS)
            by_pairs(act, pair)
            keep_g(TILES - 1, 1, 2, 3)
            keep_x1t(CHUNKS * TILES - 1, 3)
            keep_x1g(CHUNKS * TILES - 1)
            keep_h1(TILES - 2)
            for g in range(GROUPS):
                keep_g(TILES - 1, 1, 3, g)
                if g == 1:
                    keep_h2(TILES - 2)
                elif g == 2:
                    keep_y(TILES - 2)
            keep_z2(TILES - 1)
            keep_h1(TILES - 1)
            keep_h2(TILES - 1)
            keep_y(TILES - 1)

        @block.tensor
        def _(pe):
            def turn_rows(u, n, bank):
                rows = rows_sb[:, u, :].rearrange("p (r d) -> p d r", d=DIM)
                for k in range(DS):
                    last = nc.tensor.transpose(bank[0:HEIGHT, k * TILE:(k + 1) * TILE],
                                               rows[:, DS * n + k, :], ident_sb[:, :])
                last.then_inc(s_turned, 1)

            def turn_s(t, u, half):
                for k in range(2):
                    if half == 0 and k == 0:
                        pe.wait_ge(rows_repeated, 2 * (t + 1))
                    if half == 1:
                        pe.wait_ge(s_ready, 4 * t + k + 1)
                    turn_rows(u, 2 * half + k, s_ps[k])

            def weigh(c, q, s):
                pe.wait_ge(zl_ready, STEPS * c + s + 1)
                if s == 0:
                    wait(pe, x1t_ready, c - 1)
                if s == 2:
                    wait(pe, xd_ready, 2 * c)
                rows, slot = ROWS[s], (q * STEPS + s) % Z_RING
                terms = [(w0_lo, z_hi), (w0_hi, z_hi), (w0_hi, z_lo)]
                for n, (w, z) in enumerate(terms):
                    last = nc.tensor.matmul(acc[q % 2][:, :], w[0:rows, s, :], z[0:rows, slot, :],
                                            start=(s == 0 and n == 0), stop=(s == STEPS - 1 and n == 2))
                last.then_inc(w0_done, 1)

            def turn_x(u, q):
                for g in range(GROUPS):
                    b0 = (q * GROUPS + g) * GROUP
                    last = nc.tensor.transpose(xg_ps[:, g * FIELDS:(g + 1) * FIELDS],
                                               s_sb[0:FIELDS, u, b0:b0 + GROUP, :].rearrange("k b d -> k (b d)"),
                                               ident_sb[0:FIELDS, 0:FIELDS])
                last.then_inc(xg_turned, 1)

            def turn_x1(c):
                pe.wait_ge(x1t_ready, c + 1)
                wait(pe, x1g_ready, c)
                for g in range(GROUPS):
                    last = nc.tensor.transpose(turn[:, g * OUT:(g + 1) * OUT],
                                               x1t_sb[:, g * 128:(g + 1) * 128], ident_sb[:, :])
                last.then_inc(x1_turned, 1)

            def g_group(c, q, g):
                if g == 0:
                    pe.wait_ge(x1g_ready, c + 1)
                if g % 2 == 0:
                    pe.wait_ge(xd_ready, 2 * c + g // 2 + 1)
                wait(pe, g_ready, GROUPS * c + g)
                nc.tensor.matmul(g_ps[:, 0:GROUP * EXT], x1g_sb[:, g, :],
                                 xd_sb[:, q % 2, g, :, :].rearrange("p b m -> p (b m)"),
                                 start=True, stop=True).then_inc(g_done, 1)

            def sum_x2(t, u, m0, m1):
                if m0 == 0:
                    pe.wait_ge(top_ready, 5 * t + 1)
                    pe.wait_ge(g_ready, CHUNKS * GROUPS * (t + 1))
                for m in range(m0, m1):
                    last = nc.tensor.matmul(top_ps[:, 0:TILE], w1_sb[:, m, :], g_sb[:, u, m, :],
                                            start=(m == 0), stop=(m == FIELDS - 1))
                if m1 == FIELDS:
                    last.then_inc(top_done, 1)

            def hidden_1(t, u, k):
                if k == 0:
                    pe.wait_ge(top_ready, 5 * t + 2)
                h = slice(k * 128, (k + 1) * 128)
                dst = top_ps[:, k * TILE:(k + 1) * TILE]
                nc.tensor.matmul(dst, wt1_sb[:, 0, h], g_sb[:, u, FIELDS, :], start=True, stop=False)
                last = nc.tensor.matmul(dst, wt1_sb[:, 1, h], z2_sb[:, :], start=False, stop=True)
                if k == H1 // 128 - 1:
                    last.then_inc(top_done, 1)

            def hidden_2(t, k):
                if k == 0:
                    pe.wait_ge(top_ready, 5 * t + 3)
                for n in range(H1 // 128):
                    last = nc.tensor.matmul(top_ps[:, k * TILE:(k + 1) * TILE], wt2_sb[:, n, k * 128:(k + 1) * 128],
                                            h1_sb[:, n, :], start=(n == 0), stop=(n == H1 // 128 - 1))
                if k == H2 // 128 - 1:
                    last.then_inc(top_done, 1)

            def output(t):
                pe.wait_ge(top_ready, 5 * t + 5)
                for n in range(H2 // 128):
                    last = nc.tensor.matmul(top_ps[0:1, 0:TILE], wt3_sb[:, n:n + 1], h2_sb[:, n, :],
                                            start=(n == 0), stop=(n == H2 // 128 - 1))
                last.then_inc(top_done, 1)

            def last_layers(t, u, q, s, first):
                if (q, s) in SUM_AT and not (first and u == 0):
                    m0 = sum(n for at, n in SUM_AT.items() if at < (q, s))
                    sum_x2(t - 1, 1 - u, m0, m0 + SUM_AT[q, s])
                if (q, s) == H1_AT[0] and not (first and u == 0):
                    hidden_1(t - 1, 1 - u, 0)
                if first:
                    return
                if (q, s) in H1_AT[1:]:
                    hidden_1(t - 2, u, H1_AT.index((q, s)))
                if (q, s) in H2_AT:
                    hidden_2(t - 2, H2_AT.index((q, s)))
                if (q, s) == Y_AT:
                    output(t - 2)

            def chunk(i, u, q, first, last):
                t = 2 * i + u
                c = CHUNKS * t + q
                last_tile = last and u == 1
                has_before = not (first and (u, q) == (0, 0))
                tile_0 = first and u == 0

                def side(s):
                    if has_before and s == 0:
                        turn_x1(c - 1)
                    if has_before and s >= 2 and s < 6:
                        g_group(c - 1, (q - 1) % 4, s - 2)
                    if s == 2:
                        turn_x(u, q)
                    if (q, s) in TURN_AT[tile_0] and not last_tile:
                        turn_s(t + 1, 1 - u, TURN_AT[tile_0].index((q, s)))
                    last_layers(t, u, q, s, first)

                for s in range(STEPS):
                    weigh(c, q, s)
                    side(s)

            def context_part(n0, n1):
                for n in range(n0, n1):
                    wait(pe, ctx_ready, n - 1)
                    nc.tensor.matmul((g_ps, top_ps)[n % 2][:, 0:HALF], wt1_ctx[:, n // 2 * 128:(n // 2 + 1) * 128],
                                     ctx_sb[:, n % 2 * HALF:(n % 2 + 1) * HALF],
                                     start=True, stop=True).then_inc(ctx_done, 1)

            def pick_blocks():
                width = BLOCK * DIM + 1
                pe.wait_ge(hot_ready, 1)
                pe.wait_ge(small_in, 16 * small)
                pe.wait_ge(middle_set, 1)
                for n in range(banks):
                    for k in range(PER_BANK):
                        f = n * PER_BANK + k
                        blocks = tables[f].shape[0] // BLOCK
                        last = nc.tensor.matmul(hot_bank[n][:, k * width:(k + 1) * width],
                                                hot_sb[0:blocks, f * TILE:(f + 1) * TILE],
                                                small_sb[0:blocks, f, :], start=True, stop=True)
                    last.then_inc(blocks_picked, 1)

            def pair(i, first, last):
                for u in range(2):
                    for q in range(CHUNKS):
                        chunk(i, u, q, first, last)

            pick_blocks()
            pe.wait_ge(ctx_in, 32)
            context_part(0, CTX_EARLY)
            pe.wait_ge(ctx_ready, CTX_EARLY)
            pe.wait_ge(ident_in, 16)
            pe.wait_ge(rows_repeated, 2)
            pe.wait_ge(small_rows, banks)
            for n in range(4):
                turn_rows(0, n, first_s_ps[n])
            pe.wait_ge(w0_folded, 6)
            pe.wait_ge(mask_set, 2 * GROUPS)
            pe.wait_ge(top_in, 64)
            pe.wait_ge(s_ready, 4)
            context_part(CTX_EARLY, CTX_PARTS)
            pe.wait_ge(ctx_ready, CTX_PARTS)
            by_pairs(pe, pair)
            for k in range(1, 4):
                hidden_1(TILES - 2, 0, k)
            turn_x1(CHUNKS * TILES - 1)
            for g in range(GROUPS):
                g_group(CHUNKS * TILES - 1, 3, g)
                if g in (0, 1):
                    hidden_2(TILES - 2, g)
                elif g == 2:
                    output(TILES - 2)
            sum_x2(TILES - 1, 1, 0, FIELDS)
            for k in range(4):
                hidden_1(TILES - 1, 1, k)
            for k in range(2):
                hidden_2(TILES - 1, k)
            output(TILES - 1)


def _constants():
    mask = np.zeros((GROUP, DIM, GROUP), np.float32)
    for b in range(GROUP):
        mask[b, :, b] = 1
    return {"ident": np.eye(128, dtype=np.float32),
            "consts": np.concatenate([mask.reshape(128, GROUP), np.tile(np.arange(BLOCK) - (BLOCK - 1) / 2, (128, 1)),
                                      -(BLOCK * np.arange(128)[:, None] + (BLOCK - 1) / 2)], 1, dtype=np.float32)}


def kernel(**inputs):
    import concourse.bacc as _bacc
    from concourse.bass_utils import run_bass_kernel_spmd as _run

    nc = _bacc.Bacc("TRN2", target_bir_lowering=False, num_devices=1)
    tables = [np.asarray(inputs[f"tbl_{f}"]) for f in range(FIELDS)]
    order = sorted(range(FIELDS), key=lambda f: (not is_small(tables[f].shape[0]), f))
    small = sum(is_small(table.shape[0]) for table in tables)
    ids = np.asarray(inputs["ids"])[:, order]
    w0 = np.asarray(inputs["L0_rec_W0"]).reshape(FIELDS, FIELDS, OUT)[order][:, order]
    m = np.arange(FIELDS)
    pairs = [((m + turned) % FIELDS, (m + shift) % FIELDS) for k, shift in enumerate(SHIFTS)
             for turned in TURNS[:ROWS[k] // FIELDS]]
    wt1 = np.asarray(inputs["W_top1"])
    arrays = {
        "in_ctx_t": np.concatenate([np.asarray(inputs["dense_ctx"]).T, np.ones((1, BATCH), np.float32)]),
        "in_ids": ids,
        "in_small_ids": ids[:TILE, :small].T.reshape(1, -1),
        "in_w0_mn": np.concatenate([w0[a, b] for a, b in pairs]),
        "in_w0_nm": np.concatenate([w0[b, a] for k, (a, b) in enumerate(pairs) if k != 1]),
        "in_w1": np.asarray(inputs["L0_rec_W1"]).reshape(FIELDS, OUT, OUT)[order].reshape(FIELDS * OUT, OUT),
        "in_wt1": wt1[:2 * OUT], "in_wt1_rest": np.concatenate([wt1[2 * OUT:], np.asarray(inputs["b_top1"])[None]]),
        "in_wt2": np.asarray(inputs["W_top2"]), "in_bt2": np.asarray(inputs["b_top2"]).reshape(-1, 128).T,
        "in_wt3": np.asarray(inputs["W_top3"]).reshape(-1, 128).T,
    }
    arrays.update({f"in_{n}": a for n, a in _constants().items()})
    arrays.update({f"in_tbl_{n}": tables[f] for n, f in enumerate(order)})
    arrays = {n: np.ascontiguousarray(a) for n, a in arrays.items()}
    ap = {n[3:]: nc.dram_tensor(n, a.shape, mybir.dt.from_np(a.dtype), kind="ExternalInput").ap()
          for n, a in arrays.items()}
    out = nc.dram_tensor("out_y", (1, BATCH), mybir.dt.float32, kind="ExternalOutput").ap()
    build(nc, ap["ctx_t"], ap["ids"], ap["small_ids"], [ap[f"tbl_{f}"] for f in range(FIELDS)], ap["w0_mn"], ap["w0_nm"],
          ap["w1"], ap["wt1"], ap["wt1_rest"], ap["wt2"], ap["bt2"], ap["wt3"],
          ap["ident"], ap["consts"], out)
    r = _run(nc, [arrays], core_ids=[0])
    return np.asarray(r.results[0]["out_y"]).reshape(BATCH, 1)
```
